# Optimizing a Trainium2 kernel written in Bass

```python
import numpy as np
import jax
import jax.numpy as jnp

def _softmax(x, axis=-1):
    return jax.nn.softmax(x, axis=axis)

def _gelu(x):
    return jax.nn.gelu(x, approximate=True)

def _silu(x):
    return jax.nn.silu(x)

def _sigmoid(x):
    return jax.nn.sigmoid(x)

def _layernorm(x, axis=-1, eps=1e-05):
    m = jnp.mean(x, axis=axis, keepdims=True)
    v = jnp.var(x, axis=axis, keepdims=True)
    return (x - m) / jnp.sqrt(v + eps)

def _scatter_add(tgt, idx, src, axis=0):
    return tgt.at[idx].add(src)

def _segment_sum(src, seg, n):
    return jax.ops.segment_sum(src, seg, n)
kernel_name = 'mk_adaln_d1_jaxref_r8_aabf64'

def setup_inputs(seed: int=0):
    np.random.seed(seed)
    _w = jnp.asarray

    def _L0_attn_setup():
        import jax, jax.numpy as jnp
        import numpy as np
        HIDDEN = 512
        HEAD_DIM = 128
        N_Q_HEADS = 32
        N_KV_HEADS = 8
        SLIDING_WINDOW = 128
        ROPE_THETA = 10000.0
        BATCH, SEQ = (1, 256)

        def _rope(t, pos):
            d = t.shape[-1]
            half = d // 2
            inv_freq = ROPE_THETA ** (-jnp.arange(half, dtype=jnp.float32) / half)
            ang = pos[:, None].astype(jnp.float32) * inv_freq[None, :]
            cos = jnp.cos(ang)[None, :, None, :]
            sin = jnp.sin(ang)[None, :, None, :]
            t1, t2 = (t[..., :half], t[..., half:])
            return jnp.concatenate([t1 * cos - t2 * sin, t1 * sin + t2 * cos], axis=-1)
        key = jax.random.key(seed)
        ks = jax.random.split(key, 5)
        w_scale = HIDDEN ** (-0.5)
        return {'x': jax.random.normal(ks[0], (BATCH, SEQ, HIDDEN), jnp.float32), 'wq': jax.random.normal(ks[1], (HIDDEN, N_Q_HEADS * HEAD_DIM), jnp.float32) * w_scale, 'wk': jax.random.normal(ks[2], (HIDDEN, N_KV_HEADS * HEAD_DIM), jnp.float32) * w_scale, 'wv': jax.random.normal(ks[3], (HIDDEN, N_KV_HEADS * HEAD_DIM), jnp.float32) * w_scale, 'wo': jax.random.normal(ks[4], (N_Q_HEADS * HEAD_DIM, HIDDEN), jnp.float32) * w_scale}
    _L0_attn_in = _L0_attn_setup()

    def _L0_ffn_setup():
        import jax, jax.numpy as jnp
        import numpy as np
        M = 512
        K = 512

        def _make_2to4_mask(key, shape):
            scores = jax.random.normal(key, shape)
            g = scores.reshape(shape[0], shape[1] // 4, 4)
            rank = jnp.argsort(jnp.argsort(-jnp.abs(g), axis=-1), axis=-1)
            return (rank < 2).reshape(shape).astype(jnp.float32)
        key = jax.random.key(seed)
        k_x, k_w12, k_b12, k_w3, k_b3, k_m = jax.random.split(key, 6)
        x = jax.random.normal(k_x, (4, 256, K), dtype=jnp.float32)
        w12_dense = jax.random.normal(k_w12, (2 * M, K), dtype=jnp.float32) * (1.0 / np.sqrt(K))
        mask12 = _make_2to4_mask(k_m, (2 * M, K))
        w12 = w12_dense * mask12
        b12 = jax.random.normal(k_b12, (2 * M,), dtype=jnp.float32) * 0.01
        w3 = jax.random.normal(k_w3, (M, M), dtype=jnp.float32) * (1.0 / np.sqrt(M))
        b3 = jax.random.normal(k_b3, (M,), dtype=jnp.float32) * 0.01
        return {'x': x, 'w12': w12, 'b12': b12, 'w3': w3, 'b3': b3}
    _L0_ffn_in = _L0_ffn_setup()
    _L0_c = _w((lambda *s: np.random.randn(*s).astype(np.float32) * 0.05)(2, 512))
    _L0_wmod = _w((lambda *s: np.random.randn(*s).astype(np.float32) * 0.05)(512, 6 * 512) * 512 ** (-0.5))
    _d = {'L0_attn_x': _L0_attn_in['x'], 'L0_attn_wq': _L0_attn_in['wq'], 'L0_attn_wk': _L0_attn_in['wk'], 'L0_attn_wv': _L0_attn_in['wv'], 'L0_attn_wo': _L0_attn_in['wo'], 'L0_ffn_w12': _L0_ffn_in['w12'], 'L0_ffn_b12': _L0_ffn_in['b12'], 'L0_ffn_w3': _L0_ffn_in['w3'], 'L0_ffn_b3': _L0_ffn_in['b3'], 'L0_c': _L0_c, 'L0_wmod': _L0_wmod}
    _x0 = _d['L0_attn_x']
    _d['L0_attn_x'] = jax.random.normal(jax.random.fold_in(jax.random.key(seed), 1), (2, 1024, 512), dtype=_x0.dtype)
    del _x0
    return _d

def reference(L0_attn_x, L0_attn_wq, L0_attn_wk, L0_attn_wv, L0_attn_wo, L0_ffn_w12, L0_ffn_b12, L0_ffn_w3, L0_ffn_b3, L0_c, L0_wmod):

    def _L0_attn_ref(x, wq, wk, wv, wo):
        import jax, jax.numpy as jnp
        import numpy as np
        HIDDEN = 512
        HEAD_DIM = 128
        N_Q_HEADS = 32
        N_KV_HEADS = 8
        SLIDING_WINDOW = 128
        ROPE_THETA = 10000.0
        BATCH, SEQ = (1, 256)

        def _rope(t, pos):
            d = t.shape[-1]
            half = d // 2
            inv_freq = ROPE_THETA ** (-jnp.arange(half, dtype=jnp.float32) / half)
            ang = pos[:, None].astype(jnp.float32) * inv_freq[None, :]
            cos = jnp.cos(ang)[None, :, None, :]
            sin = jnp.sin(ang)[None, :, None, :]
            t1, t2 = (t[..., :half], t[..., half:])
            return jnp.concatenate([t1 * cos - t2 * sin, t1 * sin + t2 * cos], axis=-1)
        B, S, _ = x.shape
        G = N_Q_HEADS // N_KV_HEADS
        sm_scale = HEAD_DIM ** (-0.5)
        q = (x @ wq).reshape(B, S, N_Q_HEADS, HEAD_DIM)
        k = (x @ wk).reshape(B, S, N_KV_HEADS, HEAD_DIM)
        v = (x @ wv).reshape(B, S, N_KV_HEADS, HEAD_DIM)
        pos = jnp.arange(S)
        q = _rope(q, pos)
        k = _rope(k, pos)
        qg = q.reshape(B, S, N_KV_HEADS, G, HEAD_DIM)
        scores = jnp.einsum('bqhgd,bshd->bhgqs', qg, k) * sm_scale
        i = pos[:, None]
        j = pos[None, :]
        allowed = (j <= i) & (j > i - SLIDING_WINDOW)
        neg = jnp.finfo(scores.dtype).min
        scores = jnp.where(allowed[None, None, None], scores, neg)
        attn = jax.nn.softmax(scores, axis=-1)
        out = jnp.einsum('bhgqs,bshd->bqhgd', attn, v).reshape(B, S, N_Q_HEADS * HEAD_DIM)
        return out @ wo

    def _L0_ffn_ref(x, w12, b12, w3, b3):
        import jax, jax.numpy as jnp
        import numpy as np
        M = 512
        K = 512

        def _make_2to4_mask(key, shape):
            scores = jax.random.normal(key, shape)
            g = scores.reshape(shape[0], shape[1] // 4, 4)
            rank = jnp.argsort(jnp.argsort(-jnp.abs(g), axis=-1), axis=-1)
            return (rank < 2).reshape(shape).astype(jnp.float32)
        x12 = jnp.einsum('bsk,mk->bsm', x, w12) + b12
        x1, x2 = jnp.split(x12, 2, axis=-1)
        x4 = jax.nn.silu(x1) * x2
        return jnp.einsum('bsm,nm->bsn', x4, w3) + b3
    x = L0_attn_x
    mod = (_silu(L0_c) @ L0_wmod).reshape(L0_c.shape[0], 6, 1, -1)
    sa, ca, ga, sb, cb, gb = (mod[:, 0], mod[:, 1], mod[:, 2], mod[:, 3], mod[:, 4], mod[:, 5])
    ga = (2 * (ga >= 0) - 1) * jnp.maximum(jnp.abs(ga), 0.25)
    gb = (2 * (gb >= 0) - 1) * jnp.maximum(jnp.abs(gb), 0.25)
    h = _layernorm(x, axis=-1) * (1 + ca) + sa
    x = x + ga * _L0_attn_ref(h, L0_attn_wq, L0_attn_wk, L0_attn_wv, L0_attn_wo)
    h = _layernorm(x, axis=-1) * (1 + cb) + sb
    x = x + gb * _L0_ffn_ref(h, L0_ffn_w12, L0_ffn_b12, L0_ffn_w3, L0_ffn_b3)
    return x

_drawn_inputs = setup_inputs


def setup_inputs(seed=0):
    import zlib

    import numpy as np

    out = dict(_drawn_inputs(seed))
    spreads = {}
    factors = {'L0_ffn_b12': 34.713, 'L0_ffn_b3': 23.348}
    for name, (base, spread) in spreads.items():
        noise = np.random.default_rng([zlib.crc32(name.encode()), seed]).standard_normal(out[name].shape)
        drawn = base * np.exp(spread * noise) if base else spread * noise
        out[name] = jnp.asarray(drawn.astype(out[name].dtype))
    for name, factor in factors.items():
        out[name] = (out[name] * factor).astype(out[name].dtype)
    return out
```

```python
from contextlib import ExitStack

import concourse.bass as bass
from concourse import mybir

P = 128
F32 = mybir.dt.float32
F32R = mybir.dt.float32r
U8 = mybir.dt.uint8
ALU = mybir.AluOpType
ACT = mybir.ActivationFunctionType
AX = mybir.AxisListType

EPS = 1e-5
MIN_GATE = 0.25
LOWEST = -3.4028234663852886e38


class Frame:

    def __init__(self, eng, s, regs=None, least=None):
        self.eng, self.s, self.regs, self.least, self.turn = eng, s, regs, least, 0
        if regs is not None:
            for per, reg in regs["base"].items():
                eng.reg_mul(reg, s, per)

    def wait(self, sem, per, k):
        if self.regs is None:
            if per * self.s + k > 0:
                self.eng.wait_ge(sem, per * self.s + k)
            return
        assert per * self.least + k > 0, (per, k)
        reg = self.regs["tmp"][self.turn % len(self.regs["tmp"])]
        self.turn += 1
        self.eng.reg_add(reg, self.regs["base"][per], k)
        self.eng.wait_ge(sem, reg)

    def stand(self):
        if self.regs is not None:
            self.eng.nop(nofuse=True)


def loop_registers(eng, name, pers):
    return {"base": {per: eng.alloc_register(f"{name}_x{per}") for per in pers},
            "tmp": [eng.alloc_register(f"{name}_t{i}") for i in range(8)]}


def adaln_block(nc, x, wq, wk, wv, wo, w12, b12, w3, b3, cond, wmod, cos, sin, x1_spill, out):
    B, SEQ, D = x.shape
    DH = cos.shape[0]
    NKV = wk.shape[1] // DH
    G = wq.shape[1] // DH // NKV
    M = w3.shape[0]
    KT = D // P
    NT = SEQ // P
    CH = 4
    CT = CH * P
    SCALE = float(DH) ** -0.5
    assert (B, NT, KT, G, DH, M, D) == (2, 8, 4, 4, 128, 512, 512)
    STEPS = B * NKV

    with ExitStack() as ctx:
        def sb(name, shape, dt):
            return ctx.enter_context(nc.sbuf_tensor(name, shape, dt))

        def sem(name):
            return ctx.enter_context(nc.semaphore(name))

        base = {}

        def sbr(name, shape, dt):
            base[name] = nc.sbuf_base
            return sb(name, shape, dt)

        def over(name, region, offset, shape, dt):
            return nc.alloc_sbuf_tensor_at(name, shape, dt, offset=base[region] + offset)

        hT = sb("hT", [P, 2, KT, SEQ], F32R)
        wp = sb("wp", [P, 2, 6, 512], F32R)
        wos = sb("wos", [P, 2, G, D], F32R)
        qT = [sbr(f"qT{i}", [P, 2, G, CT], F32R) for i in range(2)]
        kv = sb("kv", [P, 2, 2, SEQ], F32R)
        y = sbr("y", [P, NT, D], F32)
        tab = sbr("tab", [P, 2, SEQ], F32)
        bc = sb("bc", [P, 3, B, D], F32)
        st = sb("st", [P, 5, 512], F32)
        rA = sb("rA", [P, 3, 512], F32)
        rB = sb("rB", [P, 3, 512], F32)
        pr = sb("pr", [P, 2, G, P], F32)
        pT = sb("pT", [P, 2, G, P], F32R)
        pm = sbr("pm", [P, 2, 2, G, P], F32R)
        oT = sb("oT", [P, 2, G, P], F32R)
        xin = sb("xin", [P, 2, D], F32)
        xh = sb("xh", [P, 2, D], F32)
        ident = sb("ident", [P, P], F32)
        lowest = sb("lowest", [P, P], F32)
        older = sb("older", [P, P], U8)
        modT = sb("modT", [P, 4, KT, B], F32)
        b12T = sb("b12T", [P, 8], F32)
        cT = sb("cT", [P, 3, B, KT], F32)
        csil = sb("csil", [P, KT, B], F32)
        half = sb("half", [P, 1], F32)
        stat = sb("stat", [P, 2, 6], F32)
        mv = sb("mv", [P, 2, 4], F32)
        mx = sb("mx", [P, 2, G], F32)
        nb = sb("nb", [P, 2, G], F32)
        sums = sb("sums", [P, 2, G], F32)
        rs = sb("rs", [P, 2, G], F32)
        wm = [over(f"wm{i}", r, o, [P, KT, 512], F32) for i, (r, o) in enumerate(
            [("qT0", 0), ("qT0", 8192), ("y", 0), ("qT1", 0), ("qT1", 8192), ("y", 8192)])]
        csb = over("csb", "pm", 0, [P, KT, B, P], F32)
        x1a = over("x1a", "tab", 0, [P, CH, D], F32)
        x1b = over("x1b", "pm", 0, [P, CH, D], F32)

        pS = ctx.enter_context(nc.psum_tensor("pS", [P, 1024], F32))
        pTr, pAv, pOp, pXx, pP0, pP1 = (ctx.enter_context(nc.psum_tensor(n, [P, 512], F32))
                                        for n in ("pTr", "pAv", "pOp", "pXx", "pP0", "pP1"))
        pP = [pP0, pP1]

        s_const, s_tab, s_small = sem("s_const"), sem("s_tab"), sem("s_small")
        s_wm = [sem(f"s_wm{i}") for i in range(6)]
        s_cact, s_cdve, s_mod, s_modT, s_gate, s_bc = (sem(n) for n in (
            "s_cact", "s_cdve", "s_mod", "s_modT", "s_gate", "s_bc"))
        (u_scores, u_own, u_merge, u_max, u_nbias, u_exp, u_rsum, u_norm, u_trans, u_phi, u_plo, u_mask, u_av,
         u_ohi, u_olo, u_op, u_y) = (sem(n) for n in (
             "u_scores", "u_own", "u_merge", "u_max", "u_nbias", "u_exp", "u_rsum", "u_norm", "u_trans", "u_phi",
             "u_plo", "u_mask", "u_av", "u_ohi", "u_olo", "u_op", "u_y"))
        j_pe, j_act, j_done = sem("j_pe"), sem("j_act"), sem("j_done")
        v_turn, v_half = sem("v_turn"), sem("v_half")
        r_cos, r_sin, r_sum, r_hi = sem("r_cos"), sem("r_sin"), sem("r_sum"), sem("r_hi")
        w_in = [sem(f"w_in{i}") for i in range(5)]
        w_hi, w_lo = sem("w_hi"), sem("w_lo")
        x_in = [sem(f"x_in{i}") for i in range(2)]
        l_stat, l_var, l_rstd, l_norm, l_hi = (sem(n) for n in ("l_stat", "l_var", "l_rstd", "l_norm", "l_hi"))
        s_gated, s_fin, s_zero = sem("s_gated"), sem("s_fin"), sem("s_zero")
        s_spill = [sem(f"s_spill{i}") for i in range(NT)]
        x1_in = [sem(f"x1_in{i}") for i in range(2)]
        f_pe, f_silu, f_x4, f_hi, f_lo, f_out, f_gated, f_res, f_resb = (sem(n) for n in (
            "f_pe", "f_silu", "f_x4", "f_hi", "f_lo", "f_out", "f_gated", "f_res", "f_resb"))
        s_store = [sem(f"s_store{i}") for i in range(5)]

        gate_banks = [pTr[:], pAv[:], pOp[:], pS[:, 0:512]]
        block = ctx.enter_context(nc.Block())

        SLOT = {"K": 0, "Q0": 1, "Q1": 2, "Q2": 3, "Q3": 4, "V": 5}
        JOBS_OF_U = [("K", "Q0"), ("Q1",), ("Q2", "Q3"), ("V",)]
        PER_J, PER_U, PER_W, PER_R, PER_V = 12, NT, 10, 10, 2

        def jbase(b):
            return 14 + 8 * b

        def batch_of(s0):
            return s0 // NKV

        LN0, LN_TILES = 14, 8
        FFN_JOB = jbase(1) + PER_J * STEPS - 6

        xseq = [("ln", t) for t in range(NT)]
        xseq += [("fin", 0), ("fin", 1), ("ln", 8), ("ln", 9), ("ln", 10), ("ln", 11), ("fin", 2), ("fin", 3),
                 ("fin", 4), ("fin", 5), ("ln", 12), ("ln", 13), ("ln", 14), ("ln", 15), ("fin", 6), ("fin", 7)]
        xseq += [("fin", NT + t) for t in range(NT)]
        xpos = {e: i for i, e in enumerate(xseq)}

        def x_arrived(eng, e):
            i = xpos[e]
            eng.wait_ge(x_in[i % 2], 16 * (i // 2 + 1))

        def ln_job(L):
            if L < 4:
                return L
            if L < 8:
                return 6 + L
            t7 = jbase(0) + PER_J * 7 + 6
            if L < 12:
                return t7 + L - 8
            if L < 16:
                return t7 + 10 + L - 12
            if L < 20:
                return FFN_JOB + 12 + L - 16
            return FFN_JOB + 16 + L - 20

        def ln_src(L):
            if L < 16:
                return xin[:, xpos[("ln", L)] % 2, :]
            return x1_tile(L - 16)

        def x1_tile(t):
            if t < 4:
                return x1a[:, t, :]
            if t < 8:
                return x1b[:, t - 4, :]
            return y[:, t - 8, :]

        def ln_dst(L, part):
            if L < 16:
                return hT[:, part, :, (L % 8) * P:(L % 8 + 1) * P]
            i = L - 16
            return qT[(i // 4) % 2][:, part, :, (i % 4) * P:(i % 4 + 1) * P]

        def weight_pieces(u):
            if u == 2:
                return [(6 + h, (wos[:, 0, h], wos[:, 1, h])) for h in range(G)]
            slots = {3: (0, 1, 2), 4: (3, 4), 5: (5,)}[u]
            return [(10 + i, (wp[:, 0, i, :], wp[:, 1, i, :])) for i in slots]

        @block.tensor
        def _(pe):
            def mm3(o, hi_l, lo_l, hi_r, lo_r, start, stop):
                nc.tensor.matmul(o, hi_l, hi_r, start=start, stop=False, skip_group_check=True)
                nc.tensor.matmul(o, hi_l, lo_r, start=False, stop=False, skip_group_check=True)
                return nc.tensor.matmul(o, lo_l, hi_r, start=False, stop=stop, skip_group_check=True)

            def trans(f, u):
                f.wait(u_norm, PER_U, u + 1)
                f.wait(u_phi, PER_U, u)
                f.wait(u_plo, PER_U, u)
                for h in range(G):
                    last = nc.tensor.transpose(pTr[:, h * P:(h + 1) * P], pr[:, u % 2, h, :], ident[:])
                last.then_inc(u_trans, 1)

            def scores(f, u, b):
                t = u % NT
                f.wait(j_done, PER_J, jbase(b) - 1 + (6 if t >= CH else 0) + PER_J * (u // NT))
                f.wait(u_merge, PER_U, u)
                q = qT[t // CH]
                qs = slice((t % CH) * P, (t % CH + 1) * P)
                lo = 0 if t else P
                ks = slice(t * P - P + lo, t * P + P)
                for h in range(G):
                    last = mm3(pS[:, h * 256 + lo:(h + 1) * 256], q[:, 0, h, qs], q[:, 1, h, qs],
                               kv[:, 0, 0, ks], kv[:, 1, 0, ks], True, True)
                last.then_inc(u_scores, 1)

            def p_times_v(f, u, b):
                t = u % NT
                f.wait(u_mask, PER_U, u + 1)
                f.wait(j_done, PER_J, jbase(b) + (6 if t >= CH else 0) + PER_J * (u // NT))
                for own in ((1, 0) if t else (0,)):
                    tt = t - own
                    v_hi, v_lo = (kv[:, i, 1, tt * P:(tt + 1) * P] for i in range(2))
                    last = mm3(pAv[:], v_hi, v_lo, pm[:, own, 0].rearrange("p h q -> p (h q)"),
                               pm[:, own, 1].rearrange("p h q -> p (h q)"), own == 1 or t == 0, own == 0)
                last.then_inc(u_av, 1)

            def out_proj(f, u):
                f.wait(u_olo, PER_U, u + 1)
                f.wait(w_lo, PER_W, 10 * (u // NT) + 10)
                f.wait(u_y, PER_U, u + 1)
                for h in range(G):
                    last = mm3(pOp[:], oT[:, 0, h], oT[:, 1, h], wos[:, 0, h], wos[:, 1, h], h == 0, h == G - 1)
                last.then_inc(u_op, 1)

            def bank_free(f, per, j, r=None):
                f.wait(j_act, per, j - 1)
                if r is None:
                    f.wait(j_done, per, j - 1)
                else:
                    f.wait(r_cos, PER_R, r)

            def project(f, name, ch, j, w, r=None):
                bank_free(f, PER_J, j, r)
                f.wait(w_lo, PER_W, w)
                i = SLOT[name]
                o = pP[j % 2]
                for k in range(KT):
                    last = mm3(o[:], wp[:, 0, i, k * P:(k + 1) * P], wp[:, 1, i, k * P:(k + 1) * P],
                               hT[:, 0, k, ch * CT:(ch + 1) * CT], hT[:, 1, k, ch * CT:(ch + 1) * CT],
                               k == 0, k == KT - 1)
                last.then_inc(j_pe, 1)

            def turn_v(f, j):
                f.wait(j_act, PER_J, j + 1)
                f.wait(j_done, PER_J, j - 5)
                for t in range(CH):
                    last = nc.tensor.transpose(pXx[:, t * P:(t + 1) * P], rB[:, j % 3, t * P:(t + 1) * P], ident[:])
                last.then_inc(v_turn, 1)

            def ln_transpose(L):
                j = ln_job(L)
                f0 = Frame(pe, 0)
                bank_free(f0, 0, j)
                pe.wait_ge(l_norm, L + 1)
                for k in range(KT):
                    last = nc.tensor.transpose(pP[j % 2][:, k * P:(k + 1) * P], xh[:, L % 2, k * P:(k + 1) * P],
                                               ident[:])
                last.then_inc(j_pe, 1)

            def weight_transpose(i):
                j = FFN_JOB + i
                W = 10 * STEPS + i
                bank_free(Frame(pe, 0), 0, j)
                pe.wait_ge(w_in[W % 5], 16 * (W // 5 + 1))
                for k in range(KT):
                    last = nc.tensor.transpose(pP[j % 2][:, k * P:(k + 1) * P], st[:, W % 5, k * P:(k + 1) * P],
                                               ident[:])
                last.then_inc(j_pe, 1)

            def slot_jobs(f, u, b):
                js, second = u // NT, u % NT >= CH
                for name in JOBS_OF_U[u % CH]:
                    project(f, name, 0 if second else 1,
                            jbase(b) + (6 if second else 0) + PER_J * js + SLOT[name],
                            10 * (js + second) + SLOT[name] + 1,
                            PER_R * js + (10 if second else 5) + SLOT[name] - 1 if SLOT[name] >= 2 else None)

            def slot_late(f, u, b):
                js, second = u // NT, u % NT >= CH
                if u % CH == 3:
                    turn_v(f, jbase(b) + (6 if second else 0) + PER_J * js + SLOT["V"])

            def unit_step(f, u, b, jobs, late=lambda: None, prev=True, prev2=True):
                scores(f, u, b)
                if prev2:
                    p_times_v(f, u - 2, b if u >= 2 else b - 1)
                if prev:
                    trans(f, u - 1)
                jobs()
                if prev2:
                    out_proj(f, u - 2)
                late()

            def mod_columns(kind, piece):
                pe.wait_ge(s_wm[piece], 16)
                for m in range(KT):
                    for k in range(KT):
                        last = nc.tensor.matmul(pXx[:, 8 * kind + 2 * m:8 * kind + 2 * m + 2],
                                                wm[piece][:, k, m * P:(m + 1) * P], csil[:, k, :],
                                                start=(k == 0), stop=(k == KT - 1))
                last.then_inc(s_mod, 1)

            pe.wait_ge(s_cdve, 3)
            mod_columns(0, 0)
            mod_columns(1, 1)
            pe.wait_ge(s_const, 4)
            for L in range(4):
                ln_transpose(L)
            pe.wait_ge(j_done, 4)
            f0 = Frame(pe, 0)
            for name in SLOT:
                project(f0, name, 0, 4 + SLOT[name], SLOT[name] + 1)
            turn_v(f0, 9)
            for L in range(4, 8):
                ln_transpose(L)
            pe.wait_ge(s_cdve, 5)
            for piece, gate in ((2, 0), (5, 1)):
                pe.wait_ge(s_wm[piece], 16)
                for b in range(B):
                    for k in range(KT):
                        last = nc.tensor.matmul(gate_banks[2 * gate + b], csb[:, k, b, :], wm[piece][:, k, :],
                                                start=(k == 0), stop=(k == KT - 1))
                    last.then_inc(s_gate, 1)
            pe.wait_ge(s_modT, 1)
            mod_columns(2, 3)
            mod_columns(3, 4)
            pe.wait_ge(s_bc, 4)
            pe.wait_ge(s_modT, 2)

            regs = loop_registers(pe, "pe", (PER_J, PER_U, PER_W))
            for b in range(B):
                s0 = b * NKV
                f = Frame(pe, s0)
                pe.wait_ge(j_done, ln_job(8 * b + 7) + 1)
                unit_step(f, 0, b, lambda: slot_jobs(f, 0, b), prev=b > 0, prev2=b > 0)
                unit_step(f, 1, b, lambda: slot_jobs(f, 1, b), prev2=b > 0)
                with nc.tensor.Fori(s0, s0 + NKV - 1) as s:
                    f = Frame(pe, s, regs, s0)
                    for u in range(2, NT + 2):
                        unit_step(f, u, b, lambda: slot_jobs(f, u, b), lambda: slot_late(f, u, b))
                f = Frame(pe, s0 + NKV - 1)
                for u in range(2, CH):
                    unit_step(f, u, b, lambda: slot_jobs(f, u, b), lambda: slot_late(f, u, b))
                for u in range(CH, NT):
                    def jobs():
                        if b == 0:
                            t7 = jbase(0) + PER_J * 7 + 10
                            if u == 4:
                                for L in range(8, 12):
                                    ln_transpose(L)
                            if u == 5:
                                pe.wait_ge(j_done, ln_job(11) + 1)
                            for name in {5: ("K", "Q0"), 6: ("Q1", "Q2"), 7: ("Q3", "V")}.get(u, ()):
                                project(Frame(pe, 0), name, 0, t7 + SLOT[name], 80 + SLOT[name] + 1)
                        elif u < 7:
                            for i in range(4 * (u - 4), 4 * (u - 3)):
                                weight_transpose(i)
                        else:
                            for L in range(16, 20):
                                ln_transpose(L)

                    def late():
                        if b == 0 and u == 7:
                            turn_v(Frame(pe, 0), jbase(0) + PER_J * 7 + 15)
                            for L in range(12, 16):
                                ln_transpose(L)
                    unit_step(f, u, b, jobs, late)

            def ff_up(c, mp):
                i = 4 * c + mp
                if mp == 0:
                    pe.wait_ge(j_done, ln_job(16 + 4 * c + 3) + 1)
                if i >= 2:
                    pe.wait_ge(f_silu, i - 1)
                    pe.wait_ge(f_x4, i - 1)
                banks = [pS[:, 0:512], pS[:, 512:1024]] if i % 2 == 0 else [pTr[:], pAv[:]]
                q = qT[c % 2]
                for part in range(2):
                    m = mp + 4 * part
                    for k in range(KT):
                        last = mm3(banks[part], hT[:, 0, k, m * P:(m + 1) * P], hT[:, 1, k, m * P:(m + 1) * P],
                                   q[:, 0, k, :], q[:, 1, k, :], k == 0, k == KT - 1)
                last.then_inc(f_pe, 1)

            def x4_of(c):
                return wos if c % 2 == 0 else kv[:].rearrange("p i a (m t) -> p i (a m) t", m=2)

            def ff_down(c, t):
                i = 4 * c + t
                pe.wait_ge(f_lo, 4 * c + 4)
                if i >= 2:
                    pe.wait_ge(f_gated, i - 1)
                o = [pOp, pXx][i % 2]
                x4 = x4_of(c)
                for m in range(4):
                    last = mm3(o[:], x4[:, 0, m, t * P:(t + 1) * P], x4[:, 1, m, t * P:(t + 1) * P],
                               wp[:, 0, m, :], wp[:, 1, m, :], m == 0, m == 3)
                last.then_inc(f_out, 1)

            fl = Frame(pe, STEPS)
            pe.wait_ge(j_done, FFN_JOB + 12)
            p_times_v(fl, -2, 1)
            trans(fl, -1)
            pe.wait_ge(u_merge, PER_U * STEPS)
            ff_up(0, 0)
            out_proj(fl, -2)
            p_times_v(fl, -1, 1)
            out_proj(fl, -1)
            pe.wait_ge(u_olo, PER_U * STEPS)
            pe.wait_ge(u_y, PER_U * STEPS + 1)
            for c in range(4):
                for mp in range(4):
                    if (c, mp) != (0, 0):
                        ff_up(c, mp)
                    if c > 0:
                        ff_down(c - 1, mp)
                    if c < 3:
                        ln_transpose(16 + 4 * (c + 1) + mp)
            for t in range(4):
                ff_down(3, t)

        @block.scalar
        def _(act):
            def split_weight(f, dst, W, slot):
                f.wait(w_in[slot], 32, 16 * (W // 5 + 1))
                nc.scalar.copy(dst, st[:, slot, :]).then_inc(w_hi, 1)

            def result_hi(f, u):
                f.wait(u_av, PER_U, u + 1)
                nc.scalar.copy(oT[:, 0].rearrange("p h q -> p (h q)"), pAv[:]).then_inc(u_ohi, 1)

            def p_hi(f, u):
                f.wait(u_trans, PER_U, u + 1)
                f.wait(u_mask, PER_U, u)
                nc.scalar.copy(pT[:, 0].rearrange("p h q -> p (h q)"), pTr[:]).then_inc(u_phi, 1)

            def own_tile(f, u):
                f.wait(u_scores, PER_U, u + 1)
                f.wait(u_trans, PER_U, u - 1)
                nc.scalar.copy(pr[:, u % 2], pS[:].rearrange("p (h a k) -> p h a k", h=G, a=2)[:, :, 1, :]
                               ).then_inc(u_own, 1)

            def exps(f, u):
                f.wait(u_nbias, PER_U, u + 1)
                f.wait(u_norm, PER_U, u - 1)
                for h in range(G):
                    last = nc.scalar.activation(pr[:, u % 2, h, :], pr[:, u % 2, h, :], ACT.Exp,
                                                bias=nb[:, u % 2, h:h + 1], scale=SCALE,
                                                accum_out=sums[:, u % 2, h:h + 1])
                last.then_inc(u_exp, 1)

            def swap(f, j):
                f.wait(j_pe, PER_J, j + 1)
                f.wait(j_done, PER_J, j - 2)
                r = j % 3
                nc.scalar.copy(rB[0:64, r, :], pP[j % 2][64:128, :])
                nc.scalar.copy(rB[64:128, r, :], pP[j % 2][0:64, :]).then_inc(j_act, 1)

            def rope_hi(f, name, ch, j, r):
                f.wait(r_sum, PER_R, r)
                dst = kv[:, 0, 0, ch * CT:(ch + 1) * CT] if name == "K" else qT[ch][:, 0, SLOT[name] - 1, :]
                nc.scalar.copy(dst, rA[:, j % 3, :]).then_inc(r_hi, 1)

            def v_copy(f, j):
                f.wait(j_pe, PER_J, j + 1)
                f.wait(j_done, PER_J, j - 2)
                nc.scalar.copy(rB[:, j % 3, :], pP[j % 2][:]).then_inc(j_act, 1)

            def v_hi(f, ch, v):
                f.wait(v_turn, PER_V, v)
                nc.scalar.copy(kv[:, 0, 1, ch * CT:(ch + 1) * CT], pXx[:]).then_inc(v_half, 1)

            def jobs_act(f, u, b, js=0):
                t = u % NT
                a = t < CH
                ch = 1 if a else 0
                jb = jbase(b) + (0 if a else 6) + PER_J * js
                rb = (5 if a else 10) + PER_R * js

                def sw(n):
                    swap(f, jb + SLOT[n])

                def hi(n):
                    rope_hi(f, n, ch, jb + SLOT[n], rb + SLOT[n] + 1)
                if t % CH == 0:
                    sw("K"), sw("Q0")
                elif t % CH == 1:
                    hi("K"), hi("Q0"), sw("Q1")
                elif t % CH == 2:
                    hi("Q1"), sw("Q2"), sw("Q3")
                else:
                    hi("Q2"), hi("Q3"), v_copy(f, jb + 5), v_hi(f, ch, PER_V * js + (2 if a else 3))

            def ln_act(L):
                j = ln_job(L)
                kind = 0 if L < 16 else 2
                b = (L % 16) // 8
                act.wait_ge(j_pe, j + 1)
                if j >= 3:
                    act.wait_ge(j_done, j - 2)
                for k in range(KT):
                    last = nc.scalar.activation(rA[:, j % 3, k * P:(k + 1) * P], pP[j % 2][:, k * P:(k + 1) * P],
                                                ACT.Identity, bias=modT[:, kind, k, b:b + 1],
                                                scale=modT[:, kind + 1, k, b:b + 1])
                last.then_inc(j_act, 1)
                act.wait_ge(j_act, j + 1)
                nc.scalar.copy(ln_dst(L, 0), rA[:, j % 3, :].rearrange("p (k t) -> p k t", k=KT)).then_inc(l_hi, 1)

            def weight_tr_act(i):
                j = FFN_JOB + i
                act.wait_ge(j_pe, j + 1)
                dst = hT[:, 0, :, i * P:(i + 1) * P] if i < 8 else wp[:, 0, 0:4, (i - 8) * P:(i - 7) * P]
                last = nc.scalar.copy(dst, pP[j % 2][:].rearrange("p (k t) -> p k t", k=KT))
                last.then_inc(j_act, 1)

            def splits(f, u, b):
                for k, dst in weight_pieces(u):
                    if k >= 10:
                        f.wait(j_pe, PER_J, jbase(b) + k - 10 + 1)
                    split_weight(f, dst[0], k, k % 5)

            def unit_step(f, u, b, jobs, prev=True, prev2=True, split=True):
                own_tile(f, u)
                if u == 2:
                    splits(f, u, b)
                if prev2:
                    result_hi(f, u - 2)
                if prev:
                    p_hi(f, u - 1)
                exps(f, u)
                jobs()
                if split and u in (3, 4, 5):
                    splits(f, u, b)

            for b in range(B):
                act.dma_start(cT[:, 0, b, :], cond[b].rearrange("(k p) -> p k", p=P),
                              allow_slow_non_contiguous=True).then_inc(s_small, 16)
            for i in (0, 1):
                act.dma_start(wm[i][:], wmod[:, i * D:(i + 1) * D].rearrange("(k p) n -> p k n", p=P)
                              ).then_inc(s_wm[i], 16)
            act.dma_start(tab[:, 0, :], cos).then_inc(s_tab, 16)
            act.dma_start(tab[:, 1, :], sin).then_inc(s_tab, 16)
            for b in range(B):
                act.dma_start(bc[:, 2, b, :], b3.rearrange("(a n) -> a n", a=1).broadcast_to([P, D])
                              ).then_inc(s_tab, 16)
            act.dma_start(b12T[:], b12.rearrange("(m p) -> p m", p=P),
                          allow_slow_non_contiguous=True).then_inc(s_tab, 16)
            for i in (2, 5, 3, 4):
                act.dma_start(wm[i][:], wmod[:, i * D:(i + 1) * D].rearrange("(k p) n -> p k n", p=P)
                              ).then_inc(s_wm[i], 16)
            act.wait_ge(s_small, 32)
            nc.scalar.activation(cT[:, 1], cT[:, 0], ACT.Exp, scale=-1.0).then_inc(s_cact, 1)
            f0 = Frame(act, 0)
            for k in range(5):
                split_weight(f0, wp[:, 0, k, :], k, k)
            act.wait_ge(s_modT, 1)
            for L in range(4):
                ln_act(L)
            split_weight(f0, wp[:, 0, 5, :], 5, 0)
            for name in SLOT:
                j = 4 + SLOT[name]
                if name != "V":
                    swap(f0, j)
                if name not in ("K",):
                    prev_name = list(SLOT)[SLOT[name] - 1]
                    rope_hi(f0, prev_name, 0, j - 1, SLOT[prev_name] + 1)
                if name == "V":
                    v_copy(f0, j)
                    v_hi(f0, 0, 1)
            for L in range(4, 8):
                ln_act(L)

            regs = loop_registers(act, "act", (PER_J, PER_U, PER_W, PER_V, 32))
            for b in range(B):
                s0 = b * NKV
                f = Frame(act, s0)
                unit_step(f, 0, b, lambda: jobs_act(f, 0, b), prev=s0 > 0, prev2=s0 > 0)
                unit_step(f, 1, b, lambda: jobs_act(f, 1, b), prev2=s0 > 0)
                with nc.scalar.Fori(s0, s0 + NKV - 1) as s:
                    f = Frame(act, s, regs, s0)
                    for u in range(2, NT + 2):
                        unit_step(f, u, b, lambda: jobs_act(f, u, b, js=u // NT))
                f = Frame(act, s0 + NKV - 1)
                for u in range(2, NT):
                    def jobs():
                        if u < CH:
                            jobs_act(f, u, b)
                        elif b == 0:
                            t7 = jbase(0) + PER_J * 7 + 10
                            r7 = 10 * 7 + 10
                            fz = Frame(act, 0)
                            if u == 4:
                                for L in range(8, 12):
                                    ln_act(L)
                            if u == 5:
                                swap(fz, t7), swap(fz, t7 + 1)
                            if u == 6:
                                rope_hi(fz, "K", 0, t7, r7 + 1), rope_hi(fz, "Q0", 0, t7 + 1, r7 + 2)
                                swap(fz, t7 + 2), swap(fz, t7 + 3)
                            if u == 7:
                                rope_hi(fz, "Q1", 0, t7 + 2, r7 + 3), rope_hi(fz, "Q2", 0, t7 + 3, r7 + 4)
                                swap(fz, t7 + 4)
                                rope_hi(fz, "Q3", 0, t7 + 4, r7 + 5), v_copy(fz, t7 + 5)
                                v_hi(fz, 0, PER_V * 7 + 3)
                                for L in range(12, 16):
                                    ln_act(L)
                        elif u < 7:
                            for i in range(4 * (u - 4), 4 * (u - 3)):
                                weight_tr_act(i)
                        else:
                            act.wait_ge(s_modT, 2)
                            for L in range(16, 20):
                                ln_act(L)
                    unit_step(f, u, b, jobs, split=b == 0)

            fl = Frame(act, STEPS)
            result_hi(fl, -2)
            p_hi(fl, -1)
            result_hi(fl, -1)

            def ff_act(c, mp):
                i = 4 * c + mp
                act.wait_ge(f_pe, i + 1)
                if i >= 2:
                    act.wait_ge(f_x4, i - 1)
                bank = pS[:, 0:512] if i % 2 == 0 else pTr[:]
                nc.scalar.activation(pr[:, i % 2].rearrange("p h q -> p (h q)"), bank, ACT.Silu,
                                     bias=b12T[:, mp:mp + 1]).then_inc(f_silu, 1)
                act.wait_ge(f_x4, i + 1)
                if c >= 2 and mp == 0:
                    act.wait_ge(f_out, 4 * (c - 1))
                if c == 0 and mp == 0:
                    act.wait_ge(u_op, PER_U * STEPS)
                x4 = wos if c % 2 == 0 else kv[:].rearrange("p i a (m t) -> p i (a m) t", m=2)
                nc.scalar.copy(x4[:, 0, mp, :], rB[:, i % 3, :]).then_inc(f_hi, 1)

            for c in range(4):
                for mp in range(4):
                    ff_act(c, mp)
                    if c < 3:
                        ln_act(16 + 4 * (c + 1) + mp)

        @block.vector
        def _(dve):
            def result_lo(f, u):
                f.wait(u_ohi, PER_U, u + 1)
                nc.vector.tensor_tensor(oT[:, 1].rearrange("p h q -> p (h q)"), pAv[:],
                                        oT[:, 0].rearrange("p h q -> p (h q)"), ALU.subtract).then_inc(u_olo, 1)

            def p_lo(f, u):
                f.wait(u_phi, PER_U, u + 1)
                nc.vector.tensor_tensor(pT[:, 1].rearrange("p h q -> p (h q)"), pTr[:],
                                        pT[:, 0].rearrange("p h q -> p (h q)"), ALU.subtract).then_inc(u_plo, 1)

            def merge(f, u):
                f.wait(u_own, PER_U, u + 1)
                f.stand()
                before = pS[:].rearrange("p (h a k) -> p h a k", h=G, a=2)[:, :, 0, :]
                if u % NT == 0:
                    before = lowest[:].unsqueeze(1).to_broadcast([P, G, P])
                nc.vector.copy_predicated(pr[:, u % 2], older[:].unsqueeze(1).to_broadcast([P, G, P]), before
                                          ).then_inc(u_merge, 1)
                f.wait(u_merge, PER_U, u + 1)
                nc.vector.tensor_reduce(mx[:, u % 2, :], pr[:, u % 2], AX.X, ALU.max, negate=True
                                        ).then_inc(u_max, 1)
                f.wait(u_max, PER_U, u + 1)
                nc.vector.tensor_scalar(nb[:, u % 2, :], mx[:, u % 2, :], SCALE, None, ALU.mult
                                        ).then_inc(u_nbias, 1)

            def recip(f, u):
                f.wait(u_exp, PER_U, u + 1)
                nc.vector.reciprocal(rs[:, u % 2, :], sums[:, u % 2, :]).then_inc(u_rsum, 1)

            def rope_cos(f, ch, j):
                f.wait(j_act, PER_J, j + 1)
                f.wait(j_done, PER_J, j - 2)
                nc.vector.tensor_tensor(rA[:, j % 3, :], pP[j % 2][:], tab[:, 0, ch * CT:(ch + 1) * CT],
                                        ALU.mult).then_inc(r_cos, 1)

            def rope_sum(f, j, r):
                f.wait(r_sin, PER_R, r)
                f.wait(r_cos, PER_R, r)
                nc.vector.tensor_tensor(rA[:, j % 3, :], rA[:, j % 3, :], rB[:, j % 3, :], ALU.add
                                        ).then_inc(r_sum, 1)

            def rope_lo(f, name, ch, j, r):
                f.wait(r_hi, PER_R, r)
                dst, hi = ((kv[:, i, 0, ch * CT:(ch + 1) * CT] if name == "K" else qT[ch][:, i, SLOT[name] - 1, :])
                           for i in (1, 0))
                nc.vector.tensor_tensor(dst, rA[:, j % 3, :], hi, ALU.subtract).then_inc(j_done, 1)

            def v_lo(f, ch, v):
                f.wait(v_half, PER_V, v)
                nc.vector.tensor_tensor(kv[:, 1, 1, ch * CT:(ch + 1) * CT], pXx[:],
                                        kv[:, 0, 1, ch * CT:(ch + 1) * CT], ALU.subtract).then_inc(j_done, 1)

            def add_y(f, u, b):
                t = u % NT
                f.wait(u_op, PER_U, u + 1)
                dve.wait_ge(s_zero, 1 + (NT if b else 0))
                nc.vector.tensor_tensor(y[:, t, :], y[:, t, :], pOp[:], ALU.add).then_inc(u_y, 1)

            def finish(f, u, b):
                t = u % NT
                f.wait(u_y, PER_U, u + 2)
                nc.vector.tensor_tensor(y[:, t, :], y[:, t, :], bc[:, 0, b, :], ALU.mult).then_inc(s_gated, 1)
                x_arrived(dve, ("fin", NT * b + t))
                dve.wait_ge(s_gated, NT * b + t + 1)
                nc.vector.tensor_tensor(y[:, t, :], y[:, t, :], xin[:, xpos[("fin", NT * b + t)] % 2, :],
                                        ALU.add).then_inc(s_fin, 1)

            def jobs_dve(f, u, b, mid, js=0):
                t = u % NT
                a = t < CH
                ch = 1 if a else 0
                jb = jbase(b) + (0 if a else 6) + PER_J * js
                rb = (5 if a else 10) + PER_R * js

                def cos_(n):
                    rope_cos(f, ch, jb + SLOT[n])

                def sum_(n):
                    rope_sum(f, jb + SLOT[n], rb + SLOT[n] + 1)

                def lo(n):
                    rope_lo(f, n, ch, jb + SLOT[n], rb + SLOT[n] + 1)
                if t % CH == 0:
                    mid(), cos_("K"), cos_("Q0")
                elif t % CH == 1:
                    sum_("K"), sum_("Q0"), mid(), lo("K"), lo("Q0"), cos_("Q1")
                elif t % CH == 2:
                    sum_("Q1"), mid(), lo("Q1"), cos_("Q2"), cos_("Q3")
                else:
                    sum_("Q2"), sum_("Q3"), mid(), lo("Q2"), lo("Q3")

            def late_dve(f, u, js=0):
                if u % CH == 3:
                    a = u % NT < CH
                    v_lo(f, 1 if a else 0, PER_V * js + (2 if a else 3))

            def ln_norm(L):
                if L < 16:
                    x_arrived(dve, ("ln", L))
                src = ln_src(L)
                nc.vector.bn_stats(stat[:, L % 2, :], src).then_inc(l_stat, 1)
                dve.wait_ge(l_stat, 2 * L + 1)
                nc.vector.bn_aggr(mv[:, L % 2, 0:2], stat[:, L % 2, :]).then_inc(l_stat, 1)
                dve.wait_ge(l_stat, 2 * L + 2)
                nc.vector.tensor_scalar(mv[:, L % 2, 2:3], mv[:, L % 2, 1:2], EPS, None, ALU.add
                                        ).then_inc(l_var, 1)
                dve.wait_ge(l_rstd, L + 1)
                if L >= 2:
                    dve.wait_ge(j_pe, ln_job(L - 2) + 1)
                last = nc.vector.tensor_scalar(xh[:, L % 2, :], src, mv[:, L % 2, 0:1], mv[:, L % 2, 3:4],
                                               ALU.subtract, ALU.mult)
                last.then_inc(l_norm, 1)

            def ln_lo(L):
                j = ln_job(L)
                dve.wait_ge(l_hi, L + 1)
                nc.vector.tensor_tensor(ln_dst(L, 1), rA[:, j % 3, :].rearrange("p (k t) -> p k t", k=KT),
                                        ln_dst(L, 0), ALU.subtract).then_inc(j_done, 1)

            def ln_group(Ls):
                ln_norm(Ls[0])
                for L in Ls:
                    if L + 1 in Ls:
                        ln_norm(L + 1)
                    ln_lo(L)

            def weight_tr_lo(i):
                j = FFN_JOB + i
                dve.wait_ge(j_act, j + 1)
                dst, hi = ((hT[:, a, :, i * P:(i + 1) * P] if i < 8 else wp[:, a, 0:4, (i - 8) * P:(i - 7) * P])
                           for a in (1, 0))
                nc.vector.tensor_tensor(dst, pP[j % 2][:].rearrange("p (k t) -> p k t", k=KT), hi, ALU.subtract
                                        ).then_inc(j_done, 1)

            def split_weight(f, dst, W, slot):
                f.wait(w_hi, PER_W, W + 1)
                nc.vector.tensor_tensor(dst[1], st[:, slot, :], dst[0], ALU.subtract).then_inc(w_lo, 1)

            def splits(f, u):
                for k, dst in weight_pieces(u):
                    split_weight(f, dst, k, k % 5)

            def unit_step(f, u, b, jobs, late=lambda: None, prev=True, prev2=True, fin=False, split=True):
                merge(f, u)
                if u == 2:
                    splits(f, u)
                if prev2:
                    result_lo(f, u - 2)
                if prev:
                    p_lo(f, u - 1)
                jobs(lambda: recip(f, u))
                if split and u in (3, 4, 5):
                    splits(f, u)
                if prev2:
                    b2 = b if u >= 2 else b - 1
                    add_y(f, u - 2, b2)
                    if fin:
                        finish(f, u - 2, b2)
                late()

            dve.wait_ge(s_cact, 1)
            nc.vector.tensor_scalar(cT[:, 1], cT[:, 1], 1.0, None, ALU.add).then_inc(s_cdve, 1)
            dve.wait_ge(s_cdve, 1)
            nc.vector.reciprocal(cT[:, 2], cT[:, 1]).then_inc(s_cdve, 1)
            dve.wait_ge(s_cdve, 2)
            nc.vector.tensor_tensor(csil[:].rearrange("p k b -> p b k"), cT[:, 0], cT[:, 2], ALU.mult
                                    ).then_inc(s_cdve, 1)
            dve.wait_ge(s_const, 4)
            nc.vector.tensor_copy(older[:], rA[:, 0, 0:P]).then_inc(s_cdve, 1)
            dve.wait_ge(s_cdve, 4)
            nc.vector.tensor_copy(csb[:], csil[:].unsqueeze(3).to_broadcast([P, KT, B, P])).then_inc(s_cdve, 1)

            f0 = Frame(dve, 0)
            ln_norm(0)
            ln_norm(1)
            for k in range(5):
                split_weight(f0, (wp[:, 0, k, :], wp[:, 1, k, :]), k, k)

            def mod_out(kind):
                nc.vector.tensor_copy(modT[:, kind], pXx[:, 8 * kind:8 * kind + 8].rearrange(
                    "p (k b) -> p k b", k=KT))
                return nc.vector.tensor_scalar(modT[:, kind + 1], pXx[:, 8 * kind + 8:8 * kind + 16].rearrange(
                    "p (k b) -> p k b", k=KT), 1.0, None, ALU.add)

            dve.wait_ge(s_mod, 2)
            mod_out(0).then_inc(s_modT, 1)
            ln_lo(0), ln_norm(2), ln_lo(1), ln_norm(3), ln_lo(2), ln_lo(3)
            split_weight(f0, (wp[:, 0, 5, :], wp[:, 1, 5, :]), 5, 0)
            dve.wait_ge(s_tab, 80)
            names = list(SLOT)
            for i in range(5):
                rope_cos(f0, 0, 4 + i)
                if i:
                    rope_lo(f0, names[i - 1], 0, 3 + i, i)
                rope_sum(f0, 4 + i, i + 1)
            rope_lo(f0, "Q3", 0, 8, 5)
            v_lo(f0, 0, 1)
            ln_group([4, 5, 6, 7])
            for i in range(4):
                gate, b = i // 2, i % 2
                g, mag = bc[:, gate, b, :], xh[:, i % 2, :]
                dve.wait_ge(s_gate, i + 1)
                nc.vector.tensor_scalar(g, gate_banks[i], 0.0, 0.5, ALU.is_ge, ALU.subtract).then_inc(s_cdve, 1)
                dve.wait_ge(s_cdve, 5 + 2 * i + 1)
                nc.vector.scalar_tensor_tensor(out=mag, in0=g, scalar=4.0, in1=gate_banks[i], op0=ALU.mult,
                                               op1=ALU.mult).then_inc(s_cdve, 1)
                dve.wait_ge(s_cdve, 5 + 2 * i + 2)
                nc.vector.scalar_tensor_tensor(out=g, in0=mag, scalar=2 * MIN_GATE, in1=g, op0=ALU.max,
                                               op1=ALU.mult).then_inc(s_bc, 1)
            dve.wait_ge(s_bc, 4)
            for b in range(B):
                nc.vector.tensor_tensor(bc[:, 2, b, :], bc[:, 2, b, :], bc[:, 1, b, :], ALU.mult).then_inc(s_bc, 1)
            dve.wait_ge(s_mod, 4)
            mod_out(2).then_inc(s_modT, 1)

            regs = loop_registers(dve, "dve", (PER_J, PER_U, PER_W, PER_V))
            for b in range(B):
                s0 = b * NKV
                f = Frame(dve, s0)
                for u in range(2):
                    unit_step(f, u, b, lambda mid: jobs_dve(f, u, b, mid), prev=s0 > 0 or u > 0, prev2=s0 > 0,
                              fin=b > 0)
                with nc.vector.Fori(s0, s0 + NKV - 1) as s:
                    f = Frame(dve, s, regs, s0)
                    for u in range(2, NT + 2):
                        unit_step(f, u, b, lambda mid: jobs_dve(f, u, b, mid, js=u // NT),
                                  lambda: late_dve(f, u, u // NT))
                f = Frame(dve, s0 + NKV - 1)
                for u in range(2, NT):
                    def jobs(mid):
                        if u < CH:
                            jobs_dve(f, u, b, mid)
                        elif b == 0:
                            t7 = jbase(0) + PER_J * 7 + 10
                            r7 = 10 * 7 + 10
                            fz = Frame(dve, 0)
                            if u == 4:
                                mid()
                                ln_group([8, 9, 10, 11])
                            if u == 5:
                                mid(), rope_cos(fz, 0, t7), rope_cos(fz, 0, t7 + 1)
                            if u == 6:
                                rope_sum(fz, t7, r7 + 1), rope_sum(fz, t7 + 1, r7 + 2), mid()
                                rope_lo(fz, "K", 0, t7, r7 + 1), rope_lo(fz, "Q0", 0, t7 + 1, r7 + 2)
                                rope_cos(fz, 0, t7 + 2), rope_cos(fz, 0, t7 + 3)
                            if u == 7:
                                rope_sum(fz, t7 + 2, r7 + 3), rope_sum(fz, t7 + 3, r7 + 4), mid()
                                rope_lo(fz, "Q1", 0, t7 + 2, r7 + 3), rope_lo(fz, "Q2", 0, t7 + 3, r7 + 4)
                                rope_cos(fz, 0, t7 + 4)
                                rope_sum(fz, t7 + 4, r7 + 5), rope_lo(fz, "Q3", 0, t7 + 4, r7 + 5)
                        elif u < 7:
                            mid()
                            for i in range(4 * (u - 4), 4 * (u - 3)):
                                weight_tr_lo(i)
                        else:
                            mid()
                            dve.wait_ge(x1_in[0], 16)
                            ln_group([16, 17, 18, 19])

                    def late():
                        if u < CH:
                            late_dve(f, u)
                        elif b == 0 and u == 7:
                            v_lo(Frame(dve, 0), 0, PER_V * 7 + 3)
                            ln_group([12, 13, 14, 15])
                    unit_step(f, u, b, jobs, late, fin=True, split=b == 0)

            fl = Frame(dve, STEPS)
            result_lo(fl, -2)
            p_lo(fl, -1)
            add_y(fl, -2, 1)
            finish(fl, -2, 1)
            result_lo(fl, -1)
            add_y(fl, -1, 1)
            finish(fl, -1, 1)

            def ff_x4(c, mp):
                i = 4 * c + mp
                dve.wait_ge(f_silu, i + 1)
                if i >= 3:
                    dve.wait_ge(f_hi, i - 2)
                    dve.wait_ge(f_lo, i - 2)
                bank = pS[:, 512:1024] if i % 2 == 0 else pAv[:]
                nc.vector.scalar_tensor_tensor(out=rB[:, i % 3, :], in0=bank, scalar=b12T[:, 4 + mp:5 + mp],
                                               in1=pr[:, i % 2].rearrange("p h q -> p (h q)"), op0=ALU.add,
                                               op1=ALU.mult).then_inc(f_x4, 1)

            def ff_lo(c, mp):
                i = 4 * c + mp
                dve.wait_ge(f_hi, i + 1)
                x4 = wos if c % 2 == 0 else kv[:].rearrange("p i a (m t) -> p i (a m) t", m=2)
                nc.vector.tensor_tensor(x4[:, 1, mp, :], rB[:, i % 3, :], x4[:, 0, mp, :], ALU.subtract
                                        ).then_inc(f_lo, 1)

            def ff_gate(c, t):
                i = 4 * c + t
                dve.wait_ge(f_out, i + 1)
                if i >= 5:
                    dve.wait_ge(s_store[i % 5], 16 * (i // 5))
                nc.vector.tensor_tensor(st[:, i % 5, :], [pOp, pXx][i % 2][:], bc[:, 1, i // 8, :], ALU.mult
                                        ).then_inc(f_gated, 1)

            for c in range(4):
                for mp in range(4):
                    ff_x4(c, mp)
                    if c < 3:
                        L = 16 + 4 * (c + 1) + mp
                        if L == 20:
                            dve.wait_ge(x1_in[1], 16)
                        ln_norm(L)
                    ff_lo(c, mp)
                    if c < 3:
                        ln_lo(L)
                    if c > 0:
                        ff_gate(c - 1, mp)
            for t in range(4):
                ff_gate(3, t)

        @block.gpsimd
        def _(pool):
            def mask(f, u):
                f.wait(u_plo, PER_U, u + 1)
                f.wait(u_av, PER_U, u)
                f.stand()
                for own in ((0, 1) if u % NT else (0,)):
                    for part in range(2):
                        sign, op = (1, ALU.is_ge) if own == 0 else (-1, ALU.is_gt)
                        last = nc.gpsimd.affine_select(out=pm[:, own, part], in_=pT[:, part], compare_op=op,
                                                       fill=0.0, base=0, pattern=[[0, G], [sign, P]],
                                                       channel_multiplier=-sign)
                last.then_inc(u_mask, 1)

            def normalise(f, u):
                f.wait(u_rsum, PER_U, u + 1)
                nc.gpsimd.tensor_tensor(pr[:, u % 2], pr[:, u % 2],
                                        rs[:, u % 2, :].unsqueeze(2).to_broadcast([P, G, P]), ALU.mult
                                        ).then_inc(u_norm, 1)

            def rope_sin(f, ch, j):
                f.wait(j_act, PER_J, j + 1)
                nc.gpsimd.tensor_tensor(rB[:, j % 3, :], rB[:, j % 3, :], tab[:, 1, ch * CT:(ch + 1) * CT],
                                        ALU.mult).then_inc(r_sin, 1)

            def jobs_pool(f, u, b, js=0):
                t = u % NT
                jb = jbase(b) + (0 if t < CH else 6) + PER_J * js
                for name in JOBS_OF_U[t % CH]:
                    if name != "V":
                        rope_sin(f, 1 if t < CH else 0, jb + SLOT[name])

            def ln_rstd(L):
                pool.wait_ge(l_var, L + 1)
                nc.gpsimd.tensor_tensor(mv[:, L % 2, 3:4], mv[:, L % 2, 2:3], half[:], ALU.pow).then_inc(l_rstd, 1)

            def unit_step(f, u, b, jobs, prev=True):
                if prev:
                    mask(f, u - 1)
                normalise(f, u)
                jobs()

            def spill(t):
                pool.wait_ge(s_fin, t + 1)
                pool.dma_start(x1_spill[t * P:(t + 1) * P, :], y[:, t, :]).then_inc(s_spill[t], 16)

            def clear_y(t):
                pool.wait_ge(s_spill[t], 16)
                pool.memset(y[:, t, :], 0.0).then_inc(s_zero, 1)

            def residual_bias(i):
                pool.wait_ge(l_norm, 16 + i + 1)
                pool.wait_ge(s_bc, 6)
                nc.gpsimd.tensor_tensor(x1_tile(i), x1_tile(i), bc[:, 2, i // NT, :], ALU.add).then_inc(f_resb, 1)

            pool.memset(ident[:], 0.0).then_inc(s_const, 1)
            pool.memset(rA[:, 0, 0:P], 1.0).then_inc(s_const, 1)
            pool.memset(lowest[:], LOWEST)
            pool.memset(half[:], -0.5)
            pool.wait_ge(s_const, 2)
            nc.gpsimd.affine_select(out=ident[:], in_=ident[:], compare_op=ALU.not_equal, fill=1.0, base=0,
                                    pattern=[[-1, P]], channel_multiplier=1).then_inc(s_const, 1)
            nc.gpsimd.affine_select(out=rA[:, 0, 0:P], in_=rA[:, 0, 0:P], compare_op=ALU.is_gt, fill=0.0, base=0,
                                    pattern=[[1, P]], channel_multiplier=-1).then_inc(s_const, 1)
            pool.wait_ge(s_const, 4)
            for L in range(4):
                ln_rstd(L)
            f0 = Frame(pool, 0)
            pool.wait_ge(s_tab, 80)
            for j in range(4, 9):
                rope_sin(f0, 0, j)
            for L in range(4, 8):
                ln_rstd(L)
            pool.wait_ge(s_gate, 4)
            pool.memset(y[:, 0:NT // 2], 0.0).then_inc(u_y, 1)
            pool.memset(y[:, NT // 2:NT], 0.0).then_inc(s_zero, 1)

            regs = loop_registers(pool, "pool", (PER_J, PER_U))
            for b in range(B):
                s0 = b * NKV
                f = Frame(pool, s0)
                for u in range(2):
                    unit_step(f, u, b, lambda: jobs_pool(f, u, b), prev=s0 > 0 or u > 0)
                    if b == 1:
                        spill(u + 5)
                        clear_y(u + 4)
                if b == 1:
                    spill(7)
                    clear_y(6)
                    clear_y(7)
                with nc.gpsimd.Fori(s0, s0 + NKV - 1) as s:
                    f = Frame(pool, s, regs, s0)
                    for u in range(2, NT + 2):
                        unit_step(f, u, b, lambda: jobs_pool(f, u, b, js=u // NT))
                f = Frame(pool, s0 + NKV - 1)
                for u in range(2, NT):
                    def jobs():
                        if u < CH:
                            jobs_pool(f, u, b)
                        elif b == 0:
                            t7 = jbase(0) + PER_J * 7 + 10
                            fz = Frame(pool, 0)
                            if u == 4:
                                for L in range(8, 12):
                                    ln_rstd(L)
                            for j in {5: (0, 1), 6: (2, 3), 7: (4,)}.get(u, ()):
                                rope_sin(fz, 0, t7 + j)
                            if u == 7:
                                for L in range(12, 16):
                                    ln_rstd(L)
                        elif u == 7:
                            for L in range(16, 20):
                                ln_rstd(L)
                                residual_bias(L - 16)
                    unit_step(f, u, b, jobs)
                    if b == 0 and u >= 3:
                        spill(u - 3)
                    if b == 0 and u >= 4:
                        clear_y(u - 4)
            fl = Frame(pool, STEPS)
            mask(fl, -1)

            def ff_residual(i):
                pool.wait_ge(f_gated, i + 1)
                pool.wait_ge(f_resb, i + 1)
                nc.gpsimd.tensor_tensor(st[:, i % 5, :], st[:, i % 5, :], x1_tile(i), ALU.add).then_inc(f_res, 1)

            for c in range(4):
                for mp in range(4):
                    if c < 3:
                        L = 16 + 4 * (c + 1) + mp
                        ln_rstd(L)
                        residual_bias(L - 16)
                    if c > 0:
                        ff_residual(4 * (c - 1) + mp)
            for t in range(4):
                ff_residual(12 + t)

        @block.sync
        def _(sp):
            def load_piece(f, W, src):
                slot = W % 5
                f.wait(w_lo, PER_W, W - 4)
                f.stand()
                sp.dma_start(st[:, slot, :] if src.shape[-1] == 512 and len(src.shape) == 2 else
                             st[:, slot, :].rearrange("p (k n) -> p k n", k=KT), src).then_inc(w_in[slot], 16)

            def column_piece(w, col):
                return w.rearrange("(k p) n -> p k n", p=P)[:, :, bass.ds(col, DH)]

            def load_wo(f, g):
                for h in range(G):
                    load_piece(f, 6 + h, wo[bass.ds(g * (G * DH) + h * DH, DH), :])

            def load_proj(f, g, W):
                load_piece(f, W, column_piece(wk, g * DH))
                for h in range(G):
                    load_piece(f, W + 1 + h, column_piece(wq, g * (G * DH) + h * DH))
                load_piece(f, W + 5, column_piece(wv, g * DH))

            def load_x(i):
                kind, t = xseq[i]
                if i >= 2:
                    before, tb = xseq[i - 2]
                    sp.wait_ge(l_norm if before == "ln" else s_fin, tb + 1)
                sp.dma_start(xin[:, i % 2, :], x[t // NT, (t % NT) * P:(t % NT + 1) * P, :]
                             ).then_inc(x_in[i % 2], 16)

            load_x(0), load_x(1)
            f0 = Frame(sp, 0)
            load_piece(f0, 0, column_piece(wk, 0))
            for h in range(G):
                load_piece(f0, 1 + h, column_piece(wq, h * DH))
            for i in range(2, 4):
                load_x(i)
            load_piece(f0, 5, column_piece(wv, 0))
            for i in range(4, 10):
                load_x(i)
            regs = loop_registers(sp, "sp", (PER_W,))
            for b in range(B):
                s0 = b * NKV
                with nc.sync.Fori(s0, s0 + NKV - 1) as s:
                    f = Frame(sp, s, regs, s0)
                    load_wo(f, s - s0)
                    load_proj(f, s - s0 + 1, 10)
                f = Frame(sp, s0 + NKV - 1)
                load_wo(f, NKV - 1)
                if b == 0:
                    load_proj(f, 0, 10)
                    for i in range(10, xpos[("fin", 9)] + 1):
                        load_x(i)
            for i in range(12):
                W = 10 * STEPS + i
                if W - 5 >= 10 * STEPS:
                    sp.wait_ge(j_pe, FFN_JOB + i - 5 + 1)
                else:
                    sp.wait_ge(w_lo, W - 4)
                sp.dma_start(st[:, W % 5, :], w12[i * P:(i + 1) * P, :] if i < 8 else
                             w3[(i - 8) * P:(i - 7) * P, :]).then_inc(w_in[W % 5], 16)
                for tile in {3: (10, 11), 7: (12,), 11: (13,)}.get(i, ()):
                    load_x(xpos[("fin", tile)])
            sp.wait_ge(j_done, jbase(1) + PER_J * (STEPS - 1) + 5)
            for t in range(4):
                sp.wait_ge(s_spill[t], 16)
            sp.dma_start(x1a[:], x1_spill[0:CT, :].rearrange("(t p) d -> p t d", p=P)
                         ).then_inc(x1_in[0], 16)
            for tile in (14, 15):
                load_x(xpos[("fin", tile)])
            for t in range(4, 8):
                sp.wait_ge(s_spill[t], 16)
            sp.wait_ge(u_av, PER_U * STEPS)
            sp.dma_start(x1b[:], x1_spill[CT:2 * CT, :].rearrange("(t p) d -> p t d", p=P)).then_inc(x1_in[1], 16)
            for i in range(2 * NT):
                sp.wait_ge(f_res, i + 1)
                sp.dma_start(out[i // NT, (i % NT) * P:(i % NT + 1) * P, :], st[:, i % 5, :]
                             ).then_inc(s_store[i % 5], 16)
            for i in range(5):
                sp.wait_ge(s_store[i], 16 * ((2 * NT - i + 4) // 5))


_INS = ["L0_attn_x", "L0_attn_wq", "L0_attn_wk", "L0_attn_wv", "L0_attn_wo", "L0_ffn_w12", "L0_ffn_b12", "L0_ffn_w3",
        "L0_ffn_b3", "L0_c", "L0_wmod"]


def kernel(**inputs):
    import numpy as _np
    import concourse.bacc as _bacc
    from concourse import mybir as _mybir
    from concourse.bass_utils import run_bass_kernel_spmd as _run

    nc = _bacc.Bacc("TRN2", target_bir_lowering=False, num_devices=1)
    arrays, args = {}, []

    def take(name, a):
        arrays[name] = a
        args.append(nc.dram_tensor(name, a.shape, _mybir.dt.from_np(a.dtype), kind="ExternalInput").ap())

    for name in _INS:
        take(f"in_{name}_dram", _np.ascontiguousarray(inputs[name]))
    seq, dh = inputs["L0_attn_x"].shape[1], 128
    half = dh // 2
    freq = (10000.0 ** (-_np.arange(half) / half)).astype(_np.float32)
    angle = (freq[:, None] * _np.arange(seq, dtype=_np.float32)[None, :]).astype(_np.float64)
    take("rope_cos", _np.concatenate([_np.cos(angle), _np.cos(angle)]).astype(_np.float32))
    take("rope_sin", _np.concatenate([-_np.sin(angle), _np.sin(angle)]).astype(_np.float32))
    spill = nc.dram_tensor("x1_spill", (seq, 512), _mybir.dt.float32, kind="Internal").ap()
    out = nc.dram_tensor("out_0_dram", (2, 1024, 512), _mybir.dt.float32, kind="ExternalOutput").ap()
    adaln_block(nc, *args, spill, out)
    r = _run(nc, [arrays], core_ids=[0])
    return r.results[0]["out_0_dram"]
```

```python
from contextlib import ExitStack

import concourse.bass as bass
from concourse import mybir

P = 128
F32 = mybir.dt.float32
F32R = mybir.dt.float32r
U8 = mybir.dt.uint8
ALU = mybir.AluOpType
ACT = mybir.ActivationFunctionType
AX = mybir.AxisListType

EPS = 1e-5
MIN_GATE = 0.25
LOWEST = -3.4028234663852886e38


class Frame:

    def __init__(self, eng, s, regs=None, least=None):
        self.eng, self.s, self.regs, self.least, self.turn = eng, s, regs, least, 0
        if regs is not None:
            for per, reg in regs["base"].items():
                eng.reg_mul(reg, s, per)

    def wait(self, sem, per, k):
        if self.regs is None:
            if per * self.s + k > 0:
                self.eng.wait_ge(sem, per * self.s + k)
            return
        assert per * self.least + k > 0, (per, k)
        reg = self.regs["tmp"][self.turn % len(self.regs["tmp"])]
        self.turn += 1
        self.eng.reg_add(reg, self.regs["base"][per], k)
        self.eng.wait_ge(sem, reg)

    def stand(self):
        if self.regs is not None:
            self.eng.nop(nofuse=True)


def loop_registers(eng, name, pers):
    return {"base": {per: eng.alloc_register(f"{name}_x{per}") for per in pers},
            "tmp": [eng.alloc_register(f"{name}_t{i}") for i in range(8)]}


def adaln_block(nc, x, wq, wk, wv, wo, w12, b12, w3, b3, cond, wmod, cos, sin, x1_spill, out):
    B, SEQ, D = x.shape
    DH = cos.shape[0]
    NKV = wk.shape[1] // DH
    G = wq.shape[1] // DH // NKV
    M = w3.shape[0]
    KT = D // P
    NT = SEQ // P
    CH = 4
    CT = CH * P
    SCALE = float(DH) ** -0.5
    assert (B, NT, KT, G, DH, M, D) == (2, 8, 4, 4, 128, 512, 512)
    STEPS = B * NKV

    with ExitStack() as ctx:
        def sb(name, shape, dt):
            return ctx.enter_context(nc.sbuf_tensor(name, shape, dt))

        def sem(name):
            return ctx.enter_context(nc.semaphore(name))

        base = {}

        def sbr(name, shape, dt):
            base[name] = nc.sbuf_base
            return sb(name, shape, dt)

        def over(name, region, offset, shape, dt):
            return nc.alloc_sbuf_tensor_at(name, shape, dt, offset=base[region] + offset)

        hT = sb("hT", [P, 2, KT, SEQ], F32R)
        wp = sb("wp", [P, 2, 6, 512], F32R)
        wos = sb("wos", [P, 2, G, D], F32R)
        qT = [sbr(f"qT{i}", [P, 2, G, CT], F32R) for i in range(2)]
        kv = sb("kv", [P, 2, 2, SEQ], F32R)
        y = sbr("y", [P, NT, D], F32)
        tab = sbr("tab", [P, 2, SEQ], F32)
        bc = sb("bc", [P, 3, B, D], F32)
        st = sb("st", [P, 5, 512], F32)
        rA = sb("rA", [P, 3, 512], F32)
        rB = sb("rB", [P, 3, 512], F32)
        pr = sb("pr", [P, 2, G, P], F32)
        pT = sbr("pT", [P, 2, G, P], F32R)
        pm = sbr("pm", [P, 2, 2, G, P], F32R)
        oT = sbr("oT", [P, 2, G, P], F32R)
        xin = sb("xin", [P, 2, D], F32)
        xh = sbr("xh", [P, 2, D], F32)
        ident = sb("ident", [P, P], F32)
        lowest = sb("lowest", [P, P], F32)
        older = sb("older", [P, P], U8)
        modT = sb("modT", [P, 4, KT, B], F32)
        b12T = sb("b12T", [P, 8], F32)
        cT = sb("cT", [P, 2, B, KT], F32)
        csil = sb("csil", [P, KT, B], F32)
        half = sb("half", [P, 1], F32)
        stat = sb("stat", [P, 2, 6], F32)
        mv = sb("mv", [P, 2, 4], F32)
        mx = sb("mx", [P, 2, G], F32)
        nb = sb("nb", [P, 2, G], F32)
        sums = sb("sums", [P, 2, G], F32)
        rs = sb("rs", [P, 2, G], F32)
        wm = [over(f"wm{i}", r, o, [P, KT, 512], F32) for i, (r, o) in enumerate(
            [("qT0", 0), ("qT0", 8192), ("y", 0), ("qT1", 0), ("qT1", 8192), ("y", 8192)])]
        grow = over("grow", "oT", 0, [B, 2, D], F32)
        crow = over("crow", "pT", 0, [B, 2, D], F32)
        gmag = over("gmag", "pm", 0, [B, D], F32)
        sel = over("sel", "xh", 0, [B, B, P], F32)
        c8 = over("c8", "pm", 7168, [B * KT, P], F32)
        x1a = over("x1a", "tab", 0, [P, CH, D], F32)
        x1b = over("x1b", "pm", 0, [P, CH, D], F32)

        pS = ctx.enter_context(nc.psum_tensor("pS", [P, 1024], F32))
        pTr, pAv, pOp, pXx, pP0, pP1 = (ctx.enter_context(nc.psum_tensor(n, [P, 512], F32))
                                        for n in ("pTr", "pAv", "pOp", "pXx", "pP0", "pP1"))
        pP = [pP0, pP1]

        s_const, s_tab, s_b3, s_small = sem("s_const"), sem("s_tab"), sem("s_b3"), sem("s_small")
        s_wm = [sem(f"s_wm{i}") for i in range(6)]
        s_cT, s_cact, s_cdve, s_row, s_rowc, s_mod, s_modT, s_gdve, s_gate, s_bc = (sem(n) for n in (
            "s_cT", "s_cact", "s_cdve", "s_row", "s_rowc", "s_mod", "s_modT", "s_gdve", "s_gate", "s_bc"))
        (u_scores, u_own, u_merge, u_max, u_nbias, u_exp, u_rsum, u_norm, u_trans, u_phi, u_plo, u_mask, u_av,
         u_ohi, u_olo, u_op, u_y) = (sem(n) for n in (
             "u_scores", "u_own", "u_merge", "u_max", "u_nbias", "u_exp", "u_rsum", "u_norm", "u_trans", "u_phi",
             "u_plo", "u_mask", "u_av", "u_ohi", "u_olo", "u_op", "u_y"))
        j_pe, j_act, j_done = sem("j_pe"), sem("j_act"), sem("j_done")
        v_turn, v_half = sem("v_turn"), sem("v_half")
        r_cos, r_sin, r_sum, r_hi = sem("r_cos"), sem("r_sin"), sem("r_sum"), sem("r_hi")
        w_in = [sem(f"w_in{i}") for i in range(5)]
        w_hi, w_lo = sem("w_hi"), sem("w_lo")
        x_in = [sem(f"x_in{i}") for i in range(2)]
        l_stat, l_var, l_rstd, l_norm, l_hi = (sem(n) for n in ("l_stat", "l_var", "l_rstd", "l_norm", "l_hi"))
        s_gated, s_fin, s_zero = sem("s_gated"), sem("s_fin"), sem("s_zero")
        s_spill = [sem(f"s_spill{i}") for i in range(NT)]
        x1_in = [sem(f"x1_in{i}") for i in range(2)]
        f_pe, f_silu, f_x4, f_hi, f_lo, f_out, f_gated, f_res, f_resb = (sem(n) for n in (
            "f_pe", "f_silu", "f_x4", "f_hi", "f_lo", "f_out", "f_gated", "f_res", "f_resb"))
        s_store = [sem(f"s_store{i}") for i in range(5)]

        ROW_BLOCK = [0, 1, 2, 5, 3, 4]
        row_banks = [bank[0:B, :] for bank in (pTr, pAv, pOp, pAv, pTr, pOp)]
        gate_banks = [pAv[:], pOp[:], pXx[:], pAv[:]]
        block = ctx.enter_context(nc.Block())

        SLOT = {"K": 0, "Q0": 1, "Q1": 2, "Q2": 3, "Q3": 4, "V": 5}
        JOBS_OF_U = [("K", "Q0"), ("Q1",), ("Q2", "Q3"), ("V",)]
        PER_J, PER_U, PER_W, PER_R, PER_V = 12, NT, 10, 10, 2

        def jbase(b):
            return 14 + 8 * b

        def batch_of(s0):
            return s0 // NKV

        LN0, LN_TILES = 14, 8
        FFN_JOB = jbase(1) + PER_J * STEPS - 6

        xseq = [("ln", t) for t in range(NT)]
        xseq += [("fin", 0), ("fin", 1), ("ln", 8), ("ln", 9), ("ln", 10), ("ln", 11), ("fin", 2), ("fin", 3),
                 ("fin", 4), ("fin", 5), ("ln", 12), ("ln", 13), ("ln", 14), ("ln", 15), ("fin", 6), ("fin", 7)]
        xseq += [("fin", NT + t) for t in range(NT)]
        xpos = {e: i for i, e in enumerate(xseq)}

        def x_arrived(eng, e):
            i = xpos[e]
            eng.wait_ge(x_in[i % 2], 16 * (i // 2 + 1))

        def ln_job(L):
            if L < 4:
                return L
            if L < 8:
                return 6 + L
            t7 = jbase(0) + PER_J * 7 + 6
            if L < 12:
                return t7 + L - 8
            if L < 16:
                return t7 + 10 + L - 12
            if L < 20:
                return FFN_JOB + 12 + L - 16
            return FFN_JOB + 16 + L - 20

        def ln_src(L):
            if L < 16:
                return xin[:, xpos[("ln", L)] % 2, :]
            return x1_tile(L - 16)

        def x1_tile(t):
            if t < 4:
                return x1a[:, t, :]
            if t < 8:
                return x1b[:, t - 4, :]
            return y[:, t - 8, :]

        def ln_dst(L, part):
            if L < 16:
                return hT[:, part, :, (L % 8) * P:(L % 8 + 1) * P]
            i = L - 16
            return qT[(i // 4) % 2][:, part, :, (i % 4) * P:(i % 4 + 1) * P]

        def weight_pieces(u):
            if u == 2:
                return [(6 + h, (wos[:, 0, h], wos[:, 1, h])) for h in range(G)]
            slots = {3: (0, 1, 2), 4: (3, 4), 5: (5,)}[u]
            return [(10 + i, (wp[:, 0, i, :], wp[:, 1, i, :])) for i in slots]

        @block.tensor
        def _(pe):
            def mm3(o, hi_l, lo_l, hi_r, lo_r, start, stop):
                nc.tensor.matmul(o, hi_l, hi_r, start=start, stop=False, skip_group_check=True)
                nc.tensor.matmul(o, hi_l, lo_r, start=False, stop=False, skip_group_check=True)
                return nc.tensor.matmul(o, lo_l, hi_r, start=False, stop=stop, skip_group_check=True)

            def trans(f, u):
                f.wait(u_norm, PER_U, u + 1)
                f.wait(u_phi, PER_U, u)
                f.wait(u_plo, PER_U, u)
                for h in range(G):
                    last = nc.tensor.transpose(pTr[:, h * P:(h + 1) * P], pr[:, u % 2, h, :], ident[:])
                last.then_inc(u_trans, 1)

            def scores(f, u, b):
                t = u % NT
                f.wait(j_done, PER_J, jbase(b) - 1 + (6 if t >= CH else 0) + PER_J * (u // NT))
                f.wait(u_merge, PER_U, u)
                q = qT[t // CH]
                qs = slice((t % CH) * P, (t % CH + 1) * P)
                lo = 0 if t else P
                ks = slice(t * P - P + lo, t * P + P)
                for h in range(G):
                    last = mm3(pS[:, h * 256 + lo:(h + 1) * 256], q[:, 0, h, qs], q[:, 1, h, qs],
                               kv[:, 0, 0, ks], kv[:, 1, 0, ks], True, True)
                last.then_inc(u_scores, 1)

            def p_times_v(f, u, b):
                t = u % NT
                f.wait(u_mask, PER_U, u + 1)
                f.wait(j_done, PER_J, jbase(b) + (6 if t >= CH else 0) + PER_J * (u // NT))
                for own in ((1, 0) if t else (0,)):
                    tt = t - own
                    v_hi, v_lo = (kv[:, i, 1, tt * P:(tt + 1) * P] for i in range(2))
                    last = mm3(pAv[:], v_hi, v_lo, pm[:, own, 0].rearrange("p h q -> p (h q)"),
                               pm[:, own, 1].rearrange("p h q -> p (h q)"), own == 1 or t == 0, own == 0)
                last.then_inc(u_av, 1)

            def out_proj(f, u):
                f.wait(u_olo, PER_U, u + 1)
                f.wait(w_lo, PER_W, 10 * (u // NT) + 10)
                f.wait(u_y, PER_U, u + 1)
                for h in range(G):
                    last = mm3(pOp[:], oT[:, 0, h], oT[:, 1, h], wos[:, 0, h], wos[:, 1, h], h == 0, h == G - 1)
                last.then_inc(u_op, 1)

            def bank_free(f, per, j, r=None):
                f.wait(j_act, per, j - 1)
                if r is None:
                    f.wait(j_done, per, j - 1)
                else:
                    f.wait(r_cos, PER_R, r)

            def project(f, name, ch, j, w, r=None):
                bank_free(f, PER_J, j, r)
                f.wait(w_lo, PER_W, w)
                i = SLOT[name]
                o = pP[j % 2]
                for k in range(KT):
                    last = mm3(o[:], wp[:, 0, i, k * P:(k + 1) * P], wp[:, 1, i, k * P:(k + 1) * P],
                               hT[:, 0, k, ch * CT:(ch + 1) * CT], hT[:, 1, k, ch * CT:(ch + 1) * CT],
                               k == 0, k == KT - 1)
                last.then_inc(j_pe, 1)

            def turn_v(f, j):
                f.wait(j_act, PER_J, j + 1)
                f.wait(j_done, PER_J, j - 5)
                for t in range(CH):
                    last = nc.tensor.transpose(pXx[:, t * P:(t + 1) * P], rB[:, j % 3, t * P:(t + 1) * P], ident[:])
                last.then_inc(v_turn, 1)

            def ln_transpose(L):
                j = ln_job(L)
                f0 = Frame(pe, 0)
                bank_free(f0, 0, j)
                pe.wait_ge(l_norm, L + 1)
                for k in range(KT):
                    last = nc.tensor.transpose(pP[j % 2][:, k * P:(k + 1) * P], xh[:, L % 2, k * P:(k + 1) * P],
                                               ident[:])
                last.then_inc(j_pe, 1)

            def weight_transpose(i):
                j = FFN_JOB + i
                W = 10 * STEPS + i
                bank_free(Frame(pe, 0), 0, j)
                pe.wait_ge(w_in[W % 5], 16 * (W // 5 + 1))
                for k in range(KT):
                    last = nc.tensor.transpose(pP[j % 2][:, k * P:(k + 1) * P], st[:, W % 5, k * P:(k + 1) * P],
                                               ident[:])
                last.then_inc(j_pe, 1)

            def filler(i):
                if i < 12:
                    weight_transpose(i)
                else:
                    ln_transpose(4 + i)

            def slot_jobs(f, u, b):
                js, second = u // NT, u % NT >= CH
                for name in JOBS_OF_U[u % CH]:
                    project(f, name, 0 if second else 1,
                            jbase(b) + (6 if second else 0) + PER_J * js + SLOT[name],
                            10 * (js + second) + SLOT[name] + 1,
                            PER_R * js + (10 if second else 5) + SLOT[name] - 1 if SLOT[name] >= 2 else None)

            def slot_late(f, u, b):
                js, second = u // NT, u % NT >= CH
                if u % CH == 3:
                    turn_v(f, jbase(b) + (6 if second else 0) + PER_J * js + SLOT["V"])

            def unit_step(f, u, b, jobs, late=lambda: None, prev=True, prev2=True):
                scores(f, u, b)
                if prev2:
                    p_times_v(f, u - 2, b if u >= 2 else b - 1)
                if prev:
                    trans(f, u - 1)
                jobs()
                if prev2:
                    out_proj(f, u - 2)
                late()

            def mod_row(r):
                w = ROW_BLOCK[r]
                pe.wait_ge(s_wm[w], 16)
                if r == 5:
                    pe.wait_ge(s_gdve, 3)
                for k in range(KT):
                    last = nc.tensor.matmul(row_banks[r], csil[:, k, :], wm[w][:, k, :],
                                            start=(k == 0), stop=(k == KT - 1))
                last.then_inc(s_row, 1)

            def mod_columns(kind, copied):
                for i in range(2):
                    pe.wait_ge(s_rowc, copied + i)
                    for k in range(KT):
                        at = 8 * (kind + i) + 2 * k
                        last = nc.tensor.transpose(pXx[:, at:at + B], crow[:, i, k * P:(k + 1) * P], ident[0:B, 0:B])
                last.then_inc(s_mod, 1)

            pe.wait_ge(s_const, 4)
            pe.wait_ge(s_small, 16)
            nc.tensor.transpose(pXx[:, 0:B * KT], c8[:], ident[0:B * KT, 0:B * KT]).then_inc(s_cT, 1)
            ln_transpose(0)
            ln_transpose(1)
            pe.wait_ge(s_cdve, 3)
            mod_row(0)
            mod_row(1)
            mod_columns(0, 1)
            ln_transpose(2)
            ln_transpose(3)
            pe.wait_ge(j_done, 4)
            f0 = Frame(pe, 0)
            for name in SLOT:
                project(f0, name, 0, 4 + SLOT[name], SLOT[name] + 1, SLOT[name] - 1 if SLOT[name] >= 2 else None)
            mod_row(2)
            turn_v(f0, 9)
            ln_transpose(4)
            mod_row(3)
            ln_transpose(5)
            mod_row(4)
            ln_transpose(6)
            mod_row(5)
            ln_transpose(7)

            def gates(pair):
                for i in (2 * pair, 2 * pair + 1):
                    if i == 0:
                        pe.wait_ge(s_gdve, 7)
                    if i == 2:
                        pe.wait_ge(s_modT, 2)
                    if i == 3:
                        pe.wait_ge(s_bc, 1)
                    nc.tensor.matmul(gate_banks[i], sel[:, i % 2, :], grow[:, i // 2, :], start=True, stop=True
                                     ).then_inc(s_gate, 1)

            regs = loop_registers(pe, "pe", (PER_J, PER_U, PER_W))
            for b in range(B):
                s0 = b * NKV
                f = Frame(pe, s0)

                def first_jobs(u):
                    if b == 0:
                        if u == 0:
                            pe.wait_ge(j_done, 10)
                            mod_columns(2, 3)
                        gates(u)
                    if u == 0:
                        pe.wait_ge(j_done, ln_job(8 * b + 7) + 1)
                    slot_jobs(f, u, b)
                for u in range(2):
                    unit_step(f, u, b, lambda: first_jobs(u), prev=b > 0 or u > 0, prev2=b > 0)
                if b == 0:
                    pe.wait_ge(s_bc, 4)
                with nc.tensor.Fori(s0, s0 + NKV - 1) as s:
                    f = Frame(pe, s, regs, s0)
                    for u in range(2, NT + 2):
                        unit_step(f, u, b, lambda: slot_jobs(f, u, b), lambda: slot_late(f, u, b))
                f = Frame(pe, s0 + NKV - 1)
                for u in range(2, CH):
                    unit_step(f, u, b, lambda: slot_jobs(f, u, b), lambda: slot_late(f, u, b))
                for u in range(CH, NT):
                    def jobs():
                        if b == 0:
                            t7 = jbase(0) + PER_J * 7 + 10
                            if u == 4:
                                for L in range(8, 12):
                                    ln_transpose(L)
                            if u == 5:
                                pe.wait_ge(j_done, ln_job(11) + 1)
                            for name in {5: ("K", "Q0"), 6: ("Q1", "Q2"), 7: ("Q3", "V")}.get(u, ()):
                                project(Frame(pe, 0), name, 0, t7 + SLOT[name], 80 + SLOT[name] + 1)
                        else:
                            for i in (0, 1):
                                filler(4 * (u - 4) + i)

                    def late():
                        if b == 1:
                            for i in (2, 3):
                                filler(4 * (u - 4) + i)
                        if b == 0 and u == 7:
                            turn_v(Frame(pe, 0), jbase(0) + PER_J * 7 + 15)
                            for L in range(12, 16):
                                ln_transpose(L)
                    unit_step(f, u, b, jobs, late)

            def ff_up(i, between=lambda: None):
                c, mp = i // 4, i % 4
                if mp == 0:
                    pe.wait_ge(j_done, ln_job(16 + 4 * c + 3) + 1)
                if i >= 2:
                    pe.wait_ge(f_silu, i - 1)
                    pe.wait_ge(f_x4, i - 1)
                banks = [pS[:, 0:512], pS[:, 512:1024]] if i % 2 == 0 else [pTr[:], pAv[:]]
                q = qT[c % 2]
                for part in range(2):
                    m = mp + 4 * part
                    for k in range(KT):
                        last = mm3(banks[part], hT[:, 0, k, m * P:(m + 1) * P], hT[:, 1, k, m * P:(m + 1) * P],
                                   q[:, 0, k, :], q[:, 1, k, :], k == 0, k == KT - 1)
                    if part == 0:
                        between()
                last.then_inc(f_pe, 1)

            def x4_of(c):
                return wos if c % 2 == 0 else kv[:].rearrange("p i a (m t) -> p i (a m) t", m=2)

            def ff_down(i):
                c, t = i // 4, i % 4
                pe.wait_ge(f_lo, 4 * c + 4)
                if i >= 2:
                    pe.wait_ge(f_gated, i - 1)
                o = [pOp, pXx][i % 2]
                x4 = x4_of(c)
                for m in range(4):
                    last = mm3(o[:], x4[:, 0, m, t * P:(t + 1) * P], x4[:, 1, m, t * P:(t + 1) * P],
                               wp[:, 0, m, :], wp[:, 1, m, :], m == 0, m == 3)
                last.then_inc(f_out, 1)

            fl = Frame(pe, STEPS)
            pe.wait_ge(j_done, FFN_JOB + 12)
            p_times_v(fl, -2, 1)
            trans(fl, -1)
            pe.wait_ge(u_merge, PER_U * STEPS)
            out_proj(fl, -2)
            ff_up(0)
            p_times_v(fl, -1, 1)

            def last_unit():
                out_proj(fl, -1)
                pe.wait_ge(u_y, PER_U * STEPS + 1)

            pe.wait_ge(u_plo, PER_U * STEPS)
            ff_up(1, last_unit)
            ln_transpose(20)
            ln_transpose(21)
            ff_up(2)
            ln_transpose(22)
            ln_transpose(23)
            ff_up(3)
            for i in range(4, 16):
                if i < 12:
                    ln_transpose(20 + i)
                ff_up(i)
                ff_down(i - 4)
            for i in range(12, 16):
                ff_down(i)

        @block.scalar
        def _(act):
            def split_weight(f, dst, W, slot):
                f.wait(w_in[slot], 32, 16 * (W // 5 + 1))
                nc.scalar.copy(dst, st[:, slot, :]).then_inc(w_hi, 1)

            def result_hi(f, u):
                f.wait(u_av, PER_U, u + 1)
                nc.scalar.copy(oT[:, 0].rearrange("p h q -> p (h q)"), pAv[:]).then_inc(u_ohi, 1)

            def p_hi(f, u):
                f.wait(u_trans, PER_U, u + 1)
                f.wait(u_mask, PER_U, u)
                nc.scalar.copy(pT[:, 0].rearrange("p h q -> p (h q)"), pTr[:]).then_inc(u_phi, 1)

            def own_tile(f, u):
                f.wait(u_scores, PER_U, u + 1)
                f.wait(u_trans, PER_U, u - 1)
                nc.scalar.copy(pr[:, u % 2], pS[:].rearrange("p (h a k) -> p h a k", h=G, a=2)[:, :, 1, :]
                               ).then_inc(u_own, 1)

            def exps(f, u):
                f.wait(u_nbias, PER_U, u + 1)
                f.wait(u_norm, PER_U, u - 1)
                for h in range(G):
                    last = nc.scalar.activation(pr[:, u % 2, h, :], pr[:, u % 2, h, :], ACT.Exp,
                                                bias=nb[:, u % 2, h:h + 1], scale=SCALE,
                                                accum_out=sums[:, u % 2, h:h + 1])
                last.then_inc(u_exp, 1)

            def swap(f, j):
                f.wait(j_pe, PER_J, j + 1)
                f.wait(j_done, PER_J, j - 2)
                r = j % 3
                nc.scalar.copy(rB[0:64, r, :], pP[j % 2][64:128, :])
                nc.scalar.copy(rB[64:128, r, :], pP[j % 2][0:64, :]).then_inc(j_act, 1)

            def rope_hi(f, name, ch, j, r):
                f.wait(r_sum, PER_R, r)
                dst = kv[:, 0, 0, ch * CT:(ch + 1) * CT] if name == "K" else qT[ch][:, 0, SLOT[name] - 1, :]
                nc.scalar.copy(dst, rA[:, j % 3, :]).then_inc(r_hi, 1)

            def v_copy(f, j):
                f.wait(j_pe, PER_J, j + 1)
                f.wait(j_done, PER_J, j - 2)
                nc.scalar.copy(rB[:, j % 3, :], pP[j % 2][:]).then_inc(j_act, 1)

            def v_hi(f, ch, v):
                f.wait(v_turn, PER_V, v)
                nc.scalar.copy(kv[:, 0, 1, ch * CT:(ch + 1) * CT], pXx[:]).then_inc(v_half, 1)

            def jobs_act(f, u, b, js=0):
                t = u % NT
                a = t < CH
                ch = 1 if a else 0
                jb = jbase(b) + (0 if a else 6) + PER_J * js
                rb = (5 if a else 10) + PER_R * js

                def sw(n):
                    swap(f, jb + SLOT[n])

                def hi(n):
                    rope_hi(f, n, ch, jb + SLOT[n], rb + SLOT[n] + 1)
                if t % CH == 0:
                    sw("K"), sw("Q0")
                elif t % CH == 1:
                    hi("K"), hi("Q0"), sw("Q1")
                elif t % CH == 2:
                    hi("Q1"), sw("Q2"), sw("Q3")
                else:
                    hi("Q2"), hi("Q3"), v_copy(f, jb + 5), v_hi(f, ch, PER_V * js + (2 if a else 3))

            def ln_act(L):
                j = ln_job(L)
                kind = 0 if L < 16 else 2
                b = (L % 16) // 8
                act.wait_ge(j_pe, j + 1)
                if j >= 3:
                    act.wait_ge(j_done, j - 2)
                for k in range(KT):
                    last = nc.scalar.activation(rA[:, j % 3, k * P:(k + 1) * P], pP[j % 2][:, k * P:(k + 1) * P],
                                                ACT.Identity, bias=modT[:, kind, k, b:b + 1],
                                                scale=modT[:, kind + 1, k, b:b + 1])
                last.then_inc(j_act, 1)
                act.wait_ge(j_act, j + 1)
                nc.scalar.copy(ln_dst(L, 0), rA[:, j % 3, :].rearrange("p (k t) -> p k t", k=KT)).then_inc(l_hi, 1)

            def weight_tr_act(i):
                j = FFN_JOB + i
                act.wait_ge(j_pe, j + 1)
                dst = hT[:, 0, :, i * P:(i + 1) * P] if i < 8 else wp[:, 0, 0:4, (i - 8) * P:(i - 7) * P]
                last = nc.scalar.copy(dst, pP[j % 2][:].rearrange("p (k t) -> p k t", k=KT))
                last.then_inc(j_act, 1)

            def filler(i):
                if i < 12:
                    weight_tr_act(i)
                else:
                    if i == 12:
                        act.wait_ge(s_modT, 2)
                    ln_act(4 + i)

            def splits(f, u, b):
                for k, dst in weight_pieces(u):
                    if k >= 10:
                        f.wait(j_pe, PER_J, jbase(b) + k - 10 + 1)
                    split_weight(f, dst[0], k, k % 5)

            def unit_step(f, u, b, jobs, prev=True, prev2=True, split=True):
                own_tile(f, u)
                if u == 2:
                    splits(f, u, b)
                if prev2:
                    result_hi(f, u - 2)
                if prev:
                    p_hi(f, u - 1)
                exps(f, u)
                jobs()
                if split and u in (3, 4, 5):
                    splits(f, u, b)

            act.dma_start(c8[:], cond.rearrange("b (k p) -> (b k) p", p=P)).then_inc(s_small, 16)
            for i in (0, 1):
                act.dma_start(wm[i][:], wmod[:, i * D:(i + 1) * D].rearrange("(k p) n -> p k n", p=P)
                              ).then_inc(s_wm[i], 16)
            act.wait_ge(s_cT, 1)
            nc.scalar.activation(cT[:, 0].rearrange("p b k -> p (b k)"), pXx[:, 0:B * KT], ACT.Exp, scale=-1.0
                                 ).then_inc(s_cact, 1)

            def row_copy(r, slot):
                act.wait_ge(s_row, r + 1)
                nc.scalar.copy(crow[:, slot, :], row_banks[r]).then_inc(s_rowc, 1)

            def gate_copies(pair):
                for i in (2 * pair, 2 * pair + 1):
                    act.wait_ge(s_gate, i + 1)
                    nc.scalar.copy(bc[:, i // 2, i % 2, :], gate_banks[i]).then_inc(s_bc, 1)

            f0 = Frame(act, 0)
            row_copy(0, 0)
            row_copy(1, 1)
            split_weight(f0, wp[:, 0, 0, :], 0, 0)
            act.wait_ge(s_modT, 1)
            for L in range(4):
                ln_act(L)
            for k in range(1, 6):
                split_weight(f0, wp[:, 0, k, :], k, k % 5)
            for name in SLOT:
                j = 4 + SLOT[name]
                if name != "V":
                    swap(f0, j)
                if name not in ("K",):
                    prev_name = list(SLOT)[SLOT[name] - 1]
                    rope_hi(f0, prev_name, 0, j - 1, SLOT[prev_name] + 1)
                if name == "V":
                    v_copy(f0, j)
                    v_hi(f0, 0, 1)
            for L in range(4, 7):
                ln_act(L)
            act.wait_ge(s_mod, 1)
            row_copy(4, 0)
            ln_act(7)
            row_copy(5, 1)

            regs = loop_registers(act, "act", (PER_J, PER_U, PER_W, PER_V, 32))
            for b in range(B):
                s0 = b * NKV
                f = Frame(act, s0)

                def first_jobs(u):
                    if b == 0:
                        gate_copies(u)
                    jobs_act(f, u, b)
                for u in range(2):
                    unit_step(f, u, b, lambda: first_jobs(u), prev=s0 > 0 or u > 0, prev2=s0 > 0)
                with nc.scalar.Fori(s0, s0 + NKV - 1) as s:
                    f = Frame(act, s, regs, s0)
                    for u in range(2, NT + 2):
                        unit_step(f, u, b, lambda: jobs_act(f, u, b, js=u // NT))
                f = Frame(act, s0 + NKV - 1)
                for u in range(2, NT):
                    def jobs():
                        if u < CH:
                            jobs_act(f, u, b)
                        elif b == 0:
                            t7 = jbase(0) + PER_J * 7 + 10
                            r7 = 10 * 7 + 10
                            fz = Frame(act, 0)
                            if u == 4:
                                for L in range(8, 12):
                                    ln_act(L)
                            if u == 5:
                                swap(fz, t7), swap(fz, t7 + 1)
                            if u == 6:
                                rope_hi(fz, "K", 0, t7, r7 + 1), rope_hi(fz, "Q0", 0, t7 + 1, r7 + 2)
                                swap(fz, t7 + 2), swap(fz, t7 + 3)
                            if u == 7:
                                rope_hi(fz, "Q1", 0, t7 + 2, r7 + 3), rope_hi(fz, "Q2", 0, t7 + 3, r7 + 4)
                                swap(fz, t7 + 4)
                                rope_hi(fz, "Q3", 0, t7 + 4, r7 + 5), v_copy(fz, t7 + 5)
                                v_hi(fz, 0, PER_V * 7 + 3)
                                for L in range(12, 16):
                                    ln_act(L)
                        else:
                            filler(4 * (u - 4)), filler(4 * (u - 4) + 1)
                    unit_step(f, u, b, jobs, split=b == 0)
                    if b == 1 and u >= CH:
                        filler(4 * (u - 4) + 2), filler(4 * (u - 4) + 3)

            fl = Frame(act, STEPS)
            result_hi(fl, -2)
            p_hi(fl, -1)
            result_hi(fl, -1)

            def ff_act(i):
                c, mp = i // 4, i % 4
                act.wait_ge(f_pe, i + 1)
                if i >= 2:
                    act.wait_ge(f_x4, i - 1)
                bank = pS[:, 0:512] if i % 2 == 0 else pTr[:]
                nc.scalar.activation(pr[:, i % 2].rearrange("p h q -> p (h q)"), bank, ACT.Silu,
                                     bias=b12T[:, mp:mp + 1]).then_inc(f_silu, 1)
                act.wait_ge(f_x4, i + 1)
                if c >= 2 and mp == 0:
                    act.wait_ge(f_out, 4 * (c - 1))
                if c == 0 and mp == 0:
                    act.wait_ge(u_op, PER_U * STEPS)
                x4 = wos if c % 2 == 0 else kv[:].rearrange("p i a (m t) -> p i (a m) t", m=2)
                nc.scalar.copy(x4[:, 0, mp, :], rB[:, i % 3, :]).then_inc(f_hi, 1)

            for i in range(16):
                for L in {2: (20, 21), 3: (22, 23)}.get(i, (20 + i,) if 4 <= i < 12 else ()):
                    ln_act(L)
                ff_act(i)

        @block.vector
        def _(dve):
            def result_lo(f, u):
                f.wait(u_ohi, PER_U, u + 1)
                nc.vector.tensor_tensor(oT[:, 1].rearrange("p h q -> p (h q)"), pAv[:],
                                        oT[:, 0].rearrange("p h q -> p (h q)"), ALU.subtract).then_inc(u_olo, 1)

            def p_lo(f, u):
                f.wait(u_phi, PER_U, u + 1)
                nc.vector.tensor_tensor(pT[:, 1].rearrange("p h q -> p (h q)"), pTr[:],
                                        pT[:, 0].rearrange("p h q -> p (h q)"), ALU.subtract).then_inc(u_plo, 1)

            def merge(f, u):
                f.wait(u_own, PER_U, u + 1)
                f.stand()
                before = pS[:].rearrange("p (h a k) -> p h a k", h=G, a=2)[:, :, 0, :]
                if u % NT == 0:
                    before = lowest[:].unsqueeze(1).to_broadcast([P, G, P])
                nc.vector.copy_predicated(pr[:, u % 2], older[:].unsqueeze(1).to_broadcast([P, G, P]), before
                                          ).then_inc(u_merge, 1)
                f.wait(u_merge, PER_U, u + 1)
                nc.vector.tensor_reduce(mx[:, u % 2, :], pr[:, u % 2], AX.X, ALU.max, negate=True
                                        ).then_inc(u_max, 1)
                f.wait(u_max, PER_U, u + 1)
                nc.vector.tensor_scalar(nb[:, u % 2, :], mx[:, u % 2, :], SCALE, None, ALU.mult
                                        ).then_inc(u_nbias, 1)

            def recip(f, u):
                f.wait(u_exp, PER_U, u + 1)
                nc.vector.reciprocal(rs[:, u % 2, :], sums[:, u % 2, :]).then_inc(u_rsum, 1)

            def rope_cos(f, ch, j):
                f.wait(j_act, PER_J, j + 1)
                f.wait(j_done, PER_J, j - 2)
                nc.vector.tensor_tensor(rA[:, j % 3, :], pP[j % 2][:], tab[:, 0, ch * CT:(ch + 1) * CT],
                                        ALU.mult).then_inc(r_cos, 1)

            def rope_sum(f, j, r):
                f.wait(r_sin, PER_R, r)
                f.wait(r_cos, PER_R, r)
                nc.vector.tensor_tensor(rA[:, j % 3, :], rA[:, j % 3, :], rB[:, j % 3, :], ALU.add
                                        ).then_inc(r_sum, 1)

            def rope_lo(f, name, ch, j, r):
                f.wait(r_hi, PER_R, r)
                dst, hi = ((kv[:, i, 0, ch * CT:(ch + 1) * CT] if name == "K" else qT[ch][:, i, SLOT[name] - 1, :])
                           for i in (1, 0))
                nc.vector.tensor_tensor(dst, rA[:, j % 3, :], hi, ALU.subtract).then_inc(j_done, 1)

            def v_lo(f, ch, v):
                f.wait(v_half, PER_V, v)
                nc.vector.tensor_tensor(kv[:, 1, 1, ch * CT:(ch + 1) * CT], pXx[:],
                                        kv[:, 0, 1, ch * CT:(ch + 1) * CT], ALU.subtract).then_inc(j_done, 1)

            def add_y(f, u, b):
                t = u % NT
                f.wait(u_op, PER_U, u + 1)
                dve.wait_ge(s_zero, 1 + (NT if b else 0))
                nc.vector.tensor_tensor(y[:, t, :], y[:, t, :], pOp[:], ALU.add).then_inc(u_y, 1)

            def finish(f, u, b):
                t = u % NT
                f.wait(u_y, PER_U, u + 2)
                nc.vector.tensor_tensor(y[:, t, :], y[:, t, :], bc[:, 0, b, :], ALU.mult).then_inc(s_gated, 1)
                x_arrived(dve, ("fin", NT * b + t))
                dve.wait_ge(s_gated, NT * b + t + 1)
                nc.vector.tensor_tensor(y[:, t, :], y[:, t, :], xin[:, xpos[("fin", NT * b + t)] % 2, :],
                                        ALU.add).then_inc(s_fin, 1)

            def jobs_dve(f, u, b, mid, js=0):
                t = u % NT
                a = t < CH
                ch = 1 if a else 0
                jb = jbase(b) + (0 if a else 6) + PER_J * js
                rb = (5 if a else 10) + PER_R * js

                def cos_(n):
                    rope_cos(f, ch, jb + SLOT[n])

                def sum_(n):
                    rope_sum(f, jb + SLOT[n], rb + SLOT[n] + 1)

                def lo(n):
                    rope_lo(f, n, ch, jb + SLOT[n], rb + SLOT[n] + 1)
                if t % CH == 0:
                    mid(), cos_("K"), cos_("Q0")
                elif t % CH == 1:
                    sum_("K"), sum_("Q0"), mid(), lo("K"), lo("Q0"), cos_("Q1")
                elif t % CH == 2:
                    sum_("Q1"), mid(), lo("Q1"), cos_("Q2"), cos_("Q3")
                else:
                    sum_("Q2"), sum_("Q3"), mid(), lo("Q2"), lo("Q3")

            def late_dve(f, u, js=0):
                if u % CH == 3:
                    a = u % NT < CH
                    v_lo(f, 1 if a else 0, PER_V * js + (2 if a else 3))

            def ln_stats(L):
                if L < 16:
                    x_arrived(dve, ("ln", L))
                if L in (16, 20):
                    dve.wait_ge(x1_in[L // 4 - 4], 16)
                nc.vector.bn_stats(stat[:, L % 2, :], ln_src(L)).then_inc(l_stat, 1)
                dve.wait_ge(l_stat, 2 * L + 1)
                nc.vector.bn_aggr(mv[:, L % 2, 0:2], stat[:, L % 2, :]).then_inc(l_stat, 1)
                dve.wait_ge(l_stat, 2 * L + 2)
                nc.vector.tensor_scalar(mv[:, L % 2, 2:3], mv[:, L % 2, 1:2], EPS, None, ALU.add
                                        ).then_inc(l_var, 1)

            def ln_apply(L):
                dve.wait_ge(l_rstd, L + 1)
                if L >= 2:
                    dve.wait_ge(j_pe, ln_job(L - 2) + 1)
                nc.vector.tensor_scalar(xh[:, L % 2, :], ln_src(L), mv[:, L % 2, 0:1], mv[:, L % 2, 3:4],
                                        ALU.subtract, ALU.mult).then_inc(l_norm, 1)

            def ln_norm(L):
                ln_stats(L)
                ln_apply(L)

            def ln_lo(L):
                j = ln_job(L)
                dve.wait_ge(l_hi, L + 1)
                nc.vector.tensor_tensor(ln_dst(L, 1), rA[:, j % 3, :].rearrange("p (k t) -> p k t", k=KT),
                                        ln_dst(L, 0), ALU.subtract).then_inc(j_done, 1)

            def ln_group(Ls):
                ln_norm(Ls[0])
                for L in Ls:
                    if L + 1 in Ls:
                        ln_norm(L + 1)
                    ln_lo(L)

            def weight_tr_lo(i):
                j = FFN_JOB + i
                dve.wait_ge(j_act, j + 1)
                dst, hi = ((hT[:, a, :, i * P:(i + 1) * P] if i < 8 else wp[:, a, 0:4, (i - 8) * P:(i - 7) * P])
                           for a in (1, 0))
                nc.vector.tensor_tensor(dst, pP[j % 2][:].rearrange("p (k t) -> p k t", k=KT), hi, ALU.subtract
                                        ).then_inc(j_done, 1)

            def filler(i):
                if i < 12:
                    weight_tr_lo(i)
                else:
                    ln_lo(4 + i)

            def split_weight(f, dst, W, slot):
                f.wait(w_hi, PER_W, W + 1)
                nc.vector.tensor_tensor(dst[1], st[:, slot, :], dst[0], ALU.subtract).then_inc(w_lo, 1)

            def splits(f, u):
                for k, dst in weight_pieces(u):
                    split_weight(f, dst, k, k % 5)

            def unit_step(f, u, b, jobs, late=lambda: None, prev=True, prev2=True, fin=False, split=True):
                merge(f, u)
                if u == 2:
                    splits(f, u)
                if prev2:
                    result_lo(f, u - 2)
                if prev:
                    p_lo(f, u - 1)
                jobs(lambda: recip(f, u))
                if split and u in (3, 4, 5):
                    splits(f, u)
                if prev2:
                    b2 = b if u >= 2 else b - 1
                    add_y(f, u - 2, b2)
                    if fin:
                        finish(f, u - 2, b2)
                late()

            dve.wait_ge(s_cact, 1)
            nc.vector.tensor_scalar(cT[:, 0], cT[:, 0], 1.0, None, ALU.add).then_inc(s_cdve, 1)
            dve.wait_ge(s_cdve, 1)
            nc.vector.reciprocal(cT[:, 1], cT[:, 0]).then_inc(s_cdve, 1)
            dve.wait_ge(s_cdve, 2)
            nc.vector.tensor_tensor(csil[:].rearrange("p k b -> p b k"),
                                    pXx[:, 0:B * KT].rearrange("p (b k) -> p b k", b=B), cT[:, 1], ALU.mult
                                    ).then_inc(s_cdve, 1)
            nc.vector.tensor_copy(older[:], rA[:, 2, 0:P]).then_inc(s_cdve, 1)

            f0 = Frame(dve, 0)
            for L in range(4):
                ln_norm(L)

            def mod_out(kind):
                nc.vector.tensor_copy(modT[:, kind], pXx[:, 8 * kind:8 * kind + 8].rearrange(
                    "p (k b) -> p k b", k=KT))
                return nc.vector.tensor_scalar(modT[:, kind + 1], pXx[:, 8 * kind + 8:8 * kind + 16].rearrange(
                    "p (k b) -> p k b", k=KT), 1.0, None, ALU.add)

            dve.wait_ge(s_mod, 1)
            mod_out(0).then_inc(s_modT, 1)
            split_weight(f0, (wp[:, 0, 0, :], wp[:, 1, 0, :]), 0, 0)
            for L in range(4):
                ln_lo(L)
            for k in range(1, 6):
                split_weight(f0, (wp[:, 0, k, :], wp[:, 1, k, :]), k, k % 5)
            dve.wait_ge(s_tab, 32)
            names = list(SLOT)
            for i in range(5):
                rope_cos(f0, 0, 4 + i)
                if i:
                    rope_lo(f0, names[i - 1], 0, 3 + i, i)
                rope_sum(f0, 4 + i, i + 1)
                if i in (1, 2):
                    ln_norm(3 + i)
            rope_lo(f0, "Q3", 0, 8, 5)
            v_lo(f0, 0, 1)

            def gate_row(gate):
                bank, g = row_banks[2 + gate], grow[:, gate, :]
                dve.wait_ge(s_row, gate + 3)
                nc.vector.tensor_scalar(g, bank, 0.0, 0.5, ALU.is_ge, ALU.subtract).then_inc(s_gdve, 1)
                dve.wait_ge(s_gdve, 3 * gate + 1)
                nc.vector.scalar_tensor_tensor(out=gmag[:], in0=g, scalar=4.0, in1=bank, op0=ALU.mult,
                                               op1=ALU.mult).then_inc(s_gdve, 1)
                dve.wait_ge(s_gdve, 3 * gate + 2)
                nc.vector.scalar_tensor_tensor(out=g, in0=gmag[:], scalar=2 * MIN_GATE, in1=g, op0=ALU.max,
                                               op1=ALU.mult).then_inc(s_gdve, 1)

            gate_row(0), ln_lo(4), ln_norm(6), gate_row(1), ln_lo(5), ln_norm(7), ln_lo(6), ln_lo(7)
            nc.vector.tensor_copy(sel[:], ident[0:B, 0:B].unsqueeze(2).to_broadcast([B, B, P])).then_inc(s_gdve, 1)

            regs = loop_registers(dve, "dve", (PER_J, PER_U, PER_W, PER_V))
            for b in range(B):
                s0 = b * NKV
                f = Frame(dve, s0)


                def first_jobs(u, mid):
                    if (b, u) == (0, 0):
                        dve.wait_ge(s_mod, 2)
                        mod_out(2).then_inc(s_modT, 1)
                    jobs_dve(f, u, b, mid)
                for u in range(2):
                    unit_step(f, u, b, lambda mid: first_jobs(u, mid), prev=s0 > 0 or u > 0, prev2=s0 > 0,
                              fin=b > 0)
                if b == 0:
                    dve.wait_ge(s_bc, 4)
                    dve.wait_ge(s_b3, 48)
                    for i in range(B):
                        nc.vector.tensor_tensor(bc[:, 2, i, :], bc[:, 2, i, :], bc[:, 1, i, :], ALU.mult
                                                ).then_inc(s_bc, 1)
                with nc.vector.Fori(s0, s0 + NKV - 1) as s:
                    f = Frame(dve, s, regs, s0)
                    for u in range(2, NT + 2):
                        unit_step(f, u, b, lambda mid: jobs_dve(f, u, b, mid, js=u // NT),
                                  lambda: late_dve(f, u, u // NT))
                f = Frame(dve, s0 + NKV - 1)
                for u in range(2, NT):
                    def jobs(mid):
                        if u < CH:
                            jobs_dve(f, u, b, mid)
                        elif b == 0:
                            t7 = jbase(0) + PER_J * 7 + 10
                            r7 = 10 * 7 + 10
                            fz = Frame(dve, 0)
                            if u == 4:
                                mid()
                                ln_group([8, 9, 10, 11])
                            if u == 5:
                                mid(), rope_cos(fz, 0, t7), rope_cos(fz, 0, t7 + 1)
                            if u == 6:
                                rope_sum(fz, t7, r7 + 1), rope_sum(fz, t7 + 1, r7 + 2), mid()
                                rope_lo(fz, "K", 0, t7, r7 + 1), rope_lo(fz, "Q0", 0, t7 + 1, r7 + 2)
                                rope_cos(fz, 0, t7 + 2), rope_cos(fz, 0, t7 + 3)
                            if u == 7:
                                rope_sum(fz, t7 + 2, r7 + 3), rope_sum(fz, t7 + 3, r7 + 4), mid()
                                rope_lo(fz, "Q1", 0, t7 + 2, r7 + 3), rope_lo(fz, "Q2", 0, t7 + 3, r7 + 4)
                                rope_cos(fz, 0, t7 + 4)
                                rope_sum(fz, t7 + 4, r7 + 5), rope_lo(fz, "Q3", 0, t7 + 4, r7 + 5)
                        else:
                            mid()
                            filler(4 * (u - 4)), filler(4 * (u - 4) + 1)
                            if u == 7:
                                ln_stats(18), ln_stats(19), ln_apply(18), ln_apply(19)

                    def late():
                        if u < CH:
                            late_dve(f, u)
                        elif b == 0 and u == 7:
                            v_lo(Frame(dve, 0), 0, PER_V * 7 + 3)
                            ln_group([12, 13, 14, 15])
                        elif b == 1:
                            filler(4 * (u - 4) + 2), filler(4 * (u - 4) + 3)
                            if u == 6:
                                ln_stats(16), ln_stats(17), ln_apply(16), ln_apply(17)
                    unit_step(f, u, b, jobs, late, fin=True, split=b == 0)

            fl = Frame(dve, STEPS)
            result_lo(fl, -2)
            p_lo(fl, -1)
            add_y(fl, -2, 1)
            finish(fl, -2, 1)
            result_lo(fl, -1)
            add_y(fl, -1, 1)
            finish(fl, -1, 1)

            def ff_x4(i):
                mp = i % 4
                dve.wait_ge(f_silu, i + 1)
                if i >= 3:
                    dve.wait_ge(f_hi, i - 2)
                    dve.wait_ge(f_lo, i - 2)
                bank = pS[:, 512:1024] if i % 2 == 0 else pAv[:]
                nc.vector.scalar_tensor_tensor(out=rB[:, i % 3, :], in0=bank, scalar=b12T[:, 4 + mp:5 + mp],
                                               in1=pr[:, i % 2].rearrange("p h q -> p (h q)"), op0=ALU.add,
                                               op1=ALU.mult).then_inc(f_x4, 1)

            def ff_lo(i):
                c, mp = i // 4, i % 4
                dve.wait_ge(f_hi, i + 1)
                x4 = wos if c % 2 == 0 else kv[:].rearrange("p i a (m t) -> p i (a m) t", m=2)
                nc.vector.tensor_tensor(x4[:, 1, mp, :], rB[:, i % 3, :], x4[:, 0, mp, :], ALU.subtract
                                        ).then_inc(f_lo, 1)

            def ff_gate(i):
                dve.wait_ge(f_out, i + 1)
                if i >= 5:
                    dve.wait_ge(s_store[i % 5], 16 * (i // 5))
                nc.vector.tensor_tensor(st[:, i % 5, :], [pOp, pXx][i % 2][:], bc[:, 1, i // 8, :], ALU.mult
                                        ).then_inc(f_gated, 1)

            norms = {1: (20, 21), 2: (22, 23), 3: (24,), **{i: (21 + i,) for i in range(4, 11)}}
            los = {2: (20, 21), 3: (22, 23), **{i: (20 + i,) for i in range(4, 12)}}
            for i in range(16):
                for L in norms.get(i, ()):
                    ln_stats(L)
                for L in norms.get(i, ()):
                    ln_apply(L)
                for L in los.get(i, ()):
                    ln_lo(L)
                ff_x4(i)
                ff_lo(i)
                if i >= 4:
                    ff_gate(i - 4)
            for i in range(12, 16):
                ff_gate(i)

        @block.gpsimd
        def _(pool):
            def mask(f, u):
                f.wait(u_plo, PER_U, u + 1)
                f.wait(u_av, PER_U, u)
                f.stand()
                for own in ((0, 1) if u % NT else (0,)):
                    for part in range(2):
                        sign, op = (1, ALU.is_ge) if own == 0 else (-1, ALU.is_gt)
                        last = nc.gpsimd.affine_select(out=pm[:, own, part], in_=pT[:, part], compare_op=op,
                                                       fill=0.0, base=0, pattern=[[0, G], [sign, P]],
                                                       channel_multiplier=-sign)
                last.then_inc(u_mask, 1)

            def normalise(f, u):
                f.wait(u_rsum, PER_U, u + 1)
                nc.gpsimd.tensor_tensor(pr[:, u % 2], pr[:, u % 2],
                                        rs[:, u % 2, :].unsqueeze(2).to_broadcast([P, G, P]), ALU.mult
                                        ).then_inc(u_norm, 1)

            def rope_sin(f, ch, j):
                f.wait(j_act, PER_J, j + 1)
                nc.gpsimd.tensor_tensor(rB[:, j % 3, :], rB[:, j % 3, :], tab[:, 1, ch * CT:(ch + 1) * CT],
                                        ALU.mult).then_inc(r_sin, 1)

            def jobs_pool(f, u, b, js=0):
                t = u % NT
                jb = jbase(b) + (0 if t < CH else 6) + PER_J * js
                for name in JOBS_OF_U[t % CH]:
                    if name != "V":
                        rope_sin(f, 1 if t < CH else 0, jb + SLOT[name])

            def ln_rstd(L):
                pool.wait_ge(l_var, L + 1)
                nc.gpsimd.tensor_tensor(mv[:, L % 2, 3:4], mv[:, L % 2, 2:3], half[:], ALU.pow).then_inc(l_rstd, 1)

            def unit_step(f, u, b, jobs, prev=True):
                if prev:
                    mask(f, u - 1)
                normalise(f, u)
                jobs()

            def spill(t):
                pool.wait_ge(s_fin, t + 1)
                pool.dma_start(x1_spill[t * P:(t + 1) * P, :], y[:, t, :]).then_inc(s_spill[t], 16)

            def clear_y(t):
                pool.wait_ge(s_spill[t], 16)
                pool.memset(y[:, t, :], 0.0).then_inc(s_zero, 1)

            def residual_bias(i):
                pool.wait_ge(l_norm, 16 + i + 1)
                pool.wait_ge(s_bc, 6)
                nc.gpsimd.tensor_tensor(x1_tile(i), x1_tile(i), bc[:, 2, i // NT, :], ALU.add).then_inc(f_resb, 1)

            pool.memset(ident[:], 0.0).then_inc(s_const, 1)
            pool.memset(rA[:, 2, 0:P], 1.0).then_inc(s_const, 1)
            pool.memset(lowest[:], LOWEST)
            pool.memset(half[:], -0.5)
            pool.wait_ge(s_const, 2)
            nc.gpsimd.affine_select(out=ident[:], in_=ident[:], compare_op=ALU.not_equal, fill=1.0, base=0,
                                    pattern=[[-1, P]], channel_multiplier=1).then_inc(s_const, 1)
            nc.gpsimd.affine_select(out=rA[:, 2, 0:P], in_=rA[:, 2, 0:P], compare_op=ALU.is_gt, fill=0.0, base=0,
                                    pattern=[[1, P]], channel_multiplier=-1).then_inc(s_const, 1)
            pool.wait_ge(s_const, 4)
            for L in range(4):
                ln_rstd(L)
            f0 = Frame(pool, 0)
            pool.wait_ge(s_tab, 32)
            for j in range(4, 9):
                rope_sin(f0, 0, j)
                if j in (5, 6):
                    ln_rstd(j - 1)
            ln_rstd(6)
            ln_rstd(7)
            pool.wait_ge(s_row, 4)
            pool.memset(y[:, 0:NT // 2], 0.0).then_inc(u_y, 1)
            pool.memset(y[:, NT // 2:NT], 0.0).then_inc(s_zero, 1)

            regs = loop_registers(pool, "pool", (PER_J, PER_U))
            for b in range(B):
                s0 = b * NKV
                f = Frame(pool, s0)
                for u in range(2):
                    unit_step(f, u, b, lambda: jobs_pool(f, u, b), prev=s0 > 0 or u > 0)
                    if b == 1:
                        spill(u + 5)
                        clear_y(u + 4)
                if b == 1:
                    spill(7)
                    clear_y(6)
                    clear_y(7)
                with nc.gpsimd.Fori(s0, s0 + NKV - 1) as s:
                    f = Frame(pool, s, regs, s0)
                    for u in range(2, NT + 2):
                        unit_step(f, u, b, lambda: jobs_pool(f, u, b, js=u // NT))
                f = Frame(pool, s0 + NKV - 1)
                for u in range(2, NT):
                    def jobs():
                        if u < CH:
                            jobs_pool(f, u, b)
                        elif b == 0:
                            t7 = jbase(0) + PER_J * 7 + 10
                            fz = Frame(pool, 0)
                            if u == 4:
                                for L in range(8, 12):
                                    ln_rstd(L)
                            for j in {5: (0, 1), 6: (2, 3), 7: (4,)}.get(u, ()):
                                rope_sin(fz, 0, t7 + j)
                            if u == 7:
                                for L in range(12, 16):
                                    ln_rstd(L)
                        elif u == 7:
                            ln_rstd(18), ln_rstd(19), residual_bias(2), residual_bias(3)
                    unit_step(f, u, b, jobs)
                    if b == 1 and u == 6:
                        ln_rstd(16), ln_rstd(17), residual_bias(0), residual_bias(1)
                    if b == 0 and u >= 3:
                        spill(u - 3)
                    if b == 0 and u >= 4:
                        clear_y(u - 4)
            fl = Frame(pool, STEPS)
            mask(fl, -1)

            def ff_residual(i):
                pool.wait_ge(f_gated, i + 1)
                pool.wait_ge(f_resb, i + 1)
                nc.gpsimd.tensor_tensor(st[:, i % 5, :], st[:, i % 5, :], x1_tile(i), ALU.add).then_inc(f_res, 1)

            for i in range(1, 16):
                norms = {1: (20, 21), 2: (22, 23)}.get(i, (21 + i,) if 3 <= i < 11 else ())
                for L in norms:
                    ln_rstd(L)
                for L in norms:
                    residual_bias(L - 16)
                if i >= 4:
                    ff_residual(i - 4)
            for i in range(12, 16):
                ff_residual(i)

        @block.sync
        def _(sp):
            def load_piece(f, W, src):
                slot = W % 5
                f.wait(w_lo, PER_W, W - 4)
                f.stand()
                sp.dma_start(st[:, slot, :] if src.shape[-1] == 512 and len(src.shape) == 2 else
                             st[:, slot, :].rearrange("p (k n) -> p k n", k=KT), src).then_inc(w_in[slot], 16)

            def column_piece(w, col):
                return w.rearrange("(k p) n -> p k n", p=P)[:, :, bass.ds(col, DH)]

            def load_wo(f, g):
                for h in range(G):
                    load_piece(f, 6 + h, wo[bass.ds(g * (G * DH) + h * DH, DH), :])

            def load_proj(f, g, W):
                load_piece(f, W, column_piece(wk, g * DH))
                for h in range(G):
                    load_piece(f, W + 1 + h, column_piece(wq, g * (G * DH) + h * DH))
                load_piece(f, W + 5, column_piece(wv, g * DH))

            def load_x(i):
                kind, t = xseq[i]
                if i >= 2:
                    before, tb = xseq[i - 2]
                    sp.wait_ge(l_norm if before == "ln" else s_fin, tb + 1)
                sp.dma_start(xin[:, i % 2, :], x[t // NT, (t % NT) * P:(t % NT + 1) * P, :]
                             ).then_inc(x_in[i % 2], 16)

            for i in range(4):
                load_x(i)
            f0 = Frame(sp, 0)
            load_piece(f0, 0, column_piece(wk, 0))
            for h in range(G):
                load_piece(f0, 1 + h, column_piece(wq, h * DH))
            sp.dma_start(tab[:, 0, :], cos).then_inc(s_tab, 16)
            sp.dma_start(tab[:, 1, :], sin).then_inc(s_tab, 16)
            load_x(4), load_x(5)
            load_piece(f0, 5, column_piece(wv, 0))
            for i in ROW_BLOCK[2:]:
                sp.dma_start(wm[i][:], wmod[:, i * D:(i + 1) * D].rearrange("(k p) n -> p k n", p=P)
                             ).then_inc(s_wm[i], 16)
            for b in range(B):
                sp.dma_start(bc[:, 2, b, :], b3.rearrange("(a n) -> a n", a=1).broadcast_to([P, D])
                             ).then_inc(s_b3, 16)
            sp.dma_start(b12T[:], b12.rearrange("(m p) -> p m", p=P),
                         allow_slow_non_contiguous=True).then_inc(s_b3, 16)
            for i in range(6, 10):
                load_x(i)
            regs = loop_registers(sp, "sp", (PER_W,))
            for b in range(B):
                s0 = b * NKV
                with nc.sync.Fori(s0, s0 + NKV - 1) as s:
                    f = Frame(sp, s, regs, s0)
                    load_wo(f, s - s0)
                    load_proj(f, s - s0 + 1, 10)
                f = Frame(sp, s0 + NKV - 1)
                load_wo(f, NKV - 1)
                if b == 0:
                    load_proj(f, 0, 10)
                    for i in range(10, xpos[("fin", 9)] + 1):
                        load_x(i)
            for i in range(12):
                W = 10 * STEPS + i
                if W - 5 >= 10 * STEPS:
                    sp.wait_ge(j_pe, FFN_JOB + i - 5 + 1)
                else:
                    sp.wait_ge(w_lo, W - 4)
                sp.dma_start(st[:, W % 5, :], w12[i * P:(i + 1) * P, :] if i < 8 else
                             w3[(i - 8) * P:(i - 7) * P, :]).then_inc(w_in[W % 5], 16)
                for tile in {3: (10, 11), 7: (12,), 11: (13,)}.get(i, ()):
                    load_x(xpos[("fin", tile)])
                if i == 8:
                    sp.wait_ge(j_done, jbase(1) + PER_J * (STEPS - 1) + 5)
                    for t in range(4):
                        sp.wait_ge(s_spill[t], 16)
                    sp.dma_start(x1a[:], x1_spill[0:CT, :].rearrange("(t p) d -> p t d", p=P)
                                 ).then_inc(x1_in[0], 16)
            for tile in (14, 15):
                load_x(xpos[("fin", tile)])
            for t in range(4, 8):
                sp.wait_ge(s_spill[t], 16)
            sp.wait_ge(u_av, PER_U * STEPS)
            sp.dma_start(x1b[:], x1_spill[CT:2 * CT, :].rearrange("(t p) d -> p t d", p=P)).then_inc(x1_in[1], 16)
            for i in range(2 * NT):
                sp.wait_ge(f_res, i + 1)
                sp.dma_start(out[i // NT, (i % NT) * P:(i % NT + 1) * P, :], st[:, i % 5, :]
                             ).then_inc(s_store[i % 5], 16)
            for i in range(5):
                sp.wait_ge(s_store[i], 16 * ((2 * NT - i + 4) // 5))


_INS = ["L0_attn_x", "L0_attn_wq", "L0_attn_wk", "L0_attn_wv", "L0_attn_wo", "L0_ffn_w12", "L0_ffn_b12", "L0_ffn_w3",
        "L0_ffn_b3", "L0_c", "L0_wmod"]


def kernel(**inputs):
    import numpy as _np
    import concourse.bacc as _bacc
    from concourse import mybir as _mybir
    from concourse.bass_utils import run_bass_kernel_spmd as _run

    nc = _bacc.Bacc("TRN2", target_bir_lowering=False, num_devices=1)
    arrays, args = {}, []

    def take(name, a):
        arrays[name] = a
        args.append(nc.dram_tensor(name, a.shape, _mybir.dt.from_np(a.dtype), kind="ExternalInput").ap())

    for name in _INS:
        take(f"in_{name}_dram", _np.ascontiguousarray(inputs[name]))
    seq, dh = inputs["L0_attn_x"].shape[1], 128
    half = dh // 2
    freq = (10000.0 ** (-_np.arange(half) / half)).astype(_np.float32)
    angle = (freq[:, None] * _np.arange(seq, dtype=_np.float32)[None, :]).astype(_np.float64)
    take("rope_cos", _np.concatenate([_np.cos(angle), _np.cos(angle)]).astype(_np.float32))
    take("rope_sin", _np.concatenate([-_np.sin(angle), _np.sin(angle)]).astype(_np.float32))
    spill = nc.dram_tensor("x1_spill", (seq, 512), _mybir.dt.float32, kind="Internal").ap()
    out = nc.dram_tensor("out_0_dram", (2, 1024, 512), _mybir.dt.float32, kind="ExternalOutput").ap()
    adaln_block(nc, *args, spill, out)
    r = _run(nc, [arrays], core_ids=[0])
    return r.results[0]["out_0_dram"]
```

```python
from contextlib import ExitStack

import concourse.bass as bass
from concourse import mybir

P = 128
F32 = mybir.dt.float32
F32R = mybir.dt.float32r
U8 = mybir.dt.uint8
ALU = mybir.AluOpType
ACT = mybir.ActivationFunctionType
AX = mybir.AxisListType

EPS = 1e-5
MIN_GATE = 0.25
LOWEST = -3.4028234663852886e38


class Frame:

    def __init__(self, eng, s, regs=None, least=None):
        self.eng, self.s, self.regs, self.least, self.turn = eng, s, regs, least, 0
        if regs is not None:
            for per, reg in regs["base"].items():
                eng.reg_mul(reg, s, per)

    def wait(self, sem, per, k):
        if self.regs is None:
            if per * self.s + k > 0:
                self.eng.wait_ge(sem, per * self.s + k)
            return
        assert per * self.least + k > 0, (per, k)
        reg = self.regs["tmp"][self.turn % len(self.regs["tmp"])]
        self.turn += 1
        self.eng.reg_add(reg, self.regs["base"][per], k)
        self.eng.wait_ge(sem, reg)

    def stand(self):
        if self.regs is not None:
            self.eng.nop(nofuse=True)


def loop_registers(eng, name, pers):
    return {"base": {per: eng.alloc_register(f"{name}_x{per}") for per in pers},
            "tmp": [eng.alloc_register(f"{name}_t{i}") for i in range(8)]}


def adaln_block(nc, x, wq, wk, wv, wo, w12, b12, w3, b3, cond, wmod, cos, sin, x1_spill, out):
    B, SEQ, D = x.shape
    DH = cos.shape[0]
    NKV = wk.shape[1] // DH
    G = wq.shape[1] // DH // NKV
    M = w3.shape[0]
    KT = D // P
    NT = SEQ // P
    CH = 4
    CT = CH * P
    SCALE = float(DH) ** -0.5
    assert (B, NT, KT, G, DH, M, D) == (2, 8, 4, 4, 128, 512, 512)
    STEPS = B * NKV

    with ExitStack() as ctx:
        def sb(name, shape, dt):
            return ctx.enter_context(nc.sbuf_tensor(name, shape, dt))

        def sem(name):
            return ctx.enter_context(nc.semaphore(name))

        base = {}

        def sbr(name, shape, dt):
            base[name] = nc.sbuf_base
            return sb(name, shape, dt)

        def over(name, region, offset, shape, dt):
            return nc.alloc_sbuf_tensor_at(name, shape, dt, offset=base[region] + offset)

        hT = sb("hT", [P, 2, KT, SEQ], F32R)
        wp = sb("wp", [P, 2, 6, 512], F32R)
        wos = sb("wos", [P, 2, G, D], F32R)
        qT = [sbr(f"qT{i}", [P, 2, G, CT], F32R) for i in range(2)]
        kv = sb("kv", [P, 2, 2, SEQ], F32R)
        y = sbr("y", [P, NT, D], F32)
        tab = sbr("tab", [P, 2, SEQ], F32)
        bc = sb("bc", [P, 3, B, D], F32)
        st = sb("st", [P, 5, 512], F32)
        rA = sb("rA", [P, 3, 512], F32)
        rB = sb("rB", [P, 3, 512], F32)
        pr = sb("pr", [P, 2, G, P], F32)
        pT = sbr("pT", [P, 2, G, P], F32R)
        pm = sbr("pm", [P, 2, 2, G, P], F32R)
        oT = sbr("oT", [P, 2, G, P], F32R)
        xin = sb("xin", [P, 2, D], F32)
        xh = sbr("xh", [P, 2, D], F32)
        ident = sb("ident", [P, P], F32)
        lowest = sb("lowest", [P, P], F32)
        older = sb("older", [P, P], U8)
        modT = sb("modT", [P, 4, KT, B], F32)
        b12T = sb("b12T", [P, 8], F32)
        cT = sb("cT", [P, 2, B, KT], F32)
        csil = sb("csil", [P, KT, B], F32)
        half = sb("half", [P, 1], F32)
        stat = sb("stat", [P, 2, 6], F32)
        mv = sb("mv", [P, 2, 4], F32)
        mx = sb("mx", [P, 2, G], F32)
        nb = sb("nb", [P, 2, G], F32)
        sums = sb("sums", [P, 2, G], F32)
        rs = sb("rs", [P, 2, G], F32)
        wm = [over(f"wm{i}", r, o, [P, KT, 512], F32) for i, (r, o) in enumerate(
            [("qT0", 0), ("qT0", 8192), ("y", 0), ("qT1", 0), ("qT1", 8192), ("y", 8192)])]
        grow = over("grow", "oT", 0, [B, 2, D], F32)
        crow = over("crow", "pT", 0, [B, 2, D], F32)
        gmag = over("gmag", "pm", 0, [B, D], F32)
        sel = over("sel", "xh", 0, [B, B, P], F32)
        c8 = over("c8", "pm", 7168, [B * KT, P], F32)
        x1a = over("x1a", "tab", 0, [P, CH, D], F32)
        x1b = over("x1b", "pm", 0, [P, CH, D], F32)

        pS = ctx.enter_context(nc.psum_tensor("pS", [P, 1024], F32))
        pTr, pAv, pOp, pXx, pP0, pP1 = (ctx.enter_context(nc.psum_tensor(n, [P, 512], F32))
                                        for n in ("pTr", "pAv", "pOp", "pXx", "pP0", "pP1"))
        pP = [pP0, pP1]

        s_const, s_tab, s_b3, s_c = sem("s_const"), sem("s_tab"), sem("s_b3"), sem("s_c")
        s_wm = [sem(f"s_wm{i}") for i in range(6)]
        s_cT, s_cact, s_cdve, s_row, s_rowc, s_mod, s_modT, s_gdve, s_gate, s_bc = (sem(n) for n in (
            "s_cT", "s_cact", "s_cdve", "s_row", "s_rowc", "s_mod", "s_modT", "s_gdve", "s_gate", "s_bc"))
        (u_scores, u_own, u_merge, u_max, u_nbias, u_exp, u_rsum, u_norm, u_trans, u_phi, u_plo, u_mask, u_av,
         u_ohi, u_olo, u_op, u_y) = (sem(n) for n in (
             "u_scores", "u_own", "u_merge", "u_max", "u_nbias", "u_exp", "u_rsum", "u_norm", "u_trans", "u_phi",
             "u_plo", "u_mask", "u_av", "u_ohi", "u_olo", "u_op", "u_y"))
        j_pe, j_act, j_done = sem("j_pe"), sem("j_act"), sem("j_done")
        v_turn, v_half = sem("v_turn"), sem("v_half")
        r_cos, r_sin, r_sum, r_hi = sem("r_cos"), sem("r_sin"), sem("r_sum"), sem("r_hi")
        w_in = [sem(f"w_in{i}") for i in range(5)]
        w_hi, w_lo = sem("w_hi"), sem("w_lo")
        x_in = [sem(f"x_in{i}") for i in range(2)]
        l_stat, l_var, l_rstd, l_norm, l_hi = (sem(n) for n in ("l_stat", "l_var", "l_rstd", "l_norm", "l_hi"))
        s_gated, s_fin, s_zero = sem("s_gated"), sem("s_fin"), sem("s_zero")
        s_spill = [sem(f"s_spill{i}") for i in range(NT)]
        x1_in = [sem(f"x1_in{i}") for i in range(2)]
        f_pe, f_silu, f_x4, f_hi, f_lo, f_out, f_gated, f_res, f_resb = (sem(n) for n in (
            "f_pe", "f_silu", "f_x4", "f_hi", "f_lo", "f_out", "f_gated", "f_res", "f_resb"))
        s_store = [sem(f"s_store{i}") for i in range(5)]

        ROW_BLOCK = [0, 1, 2, 5, 3, 4]
        row_banks = [bank[0:B, :] for bank in (pTr, pAv, pOp, pAv, pTr, pOp)]
        gate_banks = [pAv[:], pOp[:], pXx[:], pAv[:]]
        block = ctx.enter_context(nc.Block())

        SLOT = {"K": 0, "Q0": 1, "Q1": 2, "Q2": 3, "Q3": 4, "V": 5}
        JOBS_OF_U = [("K", "Q0"), ("Q1",), ("Q2", "Q3"), ("V",)]
        PER_J, PER_U, PER_W, PER_R, PER_V = 12, NT, 10, 10, 2

        def jbase(b):
            return 14 + 8 * b

        def batch_of(s0):
            return s0 // NKV

        LN0, LN_TILES = 14, 8
        FFN_JOB = jbase(1) + PER_J * STEPS - 6

        xseq = [("ln", t) for t in range(NT)]
        xseq += [("ln", 8), ("fin", 0), ("ln", 9), ("fin", 1), ("ln", 10), ("ln", 11), ("fin", 2), ("ln", 12),
                 ("fin", 3), ("ln", 13), ("fin", 4), ("ln", 14), ("ln", 15), ("fin", 5), ("fin", 6), ("fin", 7)]
        xseq += [("fin", NT + t) for t in range(NT)]
        xpos = {e: i for i, e in enumerate(xseq)}

        def x_arrived(eng, e):
            i = xpos[e]
            eng.wait_ge(x_in[i % 2], 16 * (i // 2 + 1))

        TURN = [8, 9, 10, 11, "K", "Q0", 12, "Q1", "Q2", 13, "Q3", "V", 14, 15]
        TURN_NOW = {4: (9, 10), 5: ("K", "Q0"), 6: ("Q1", "Q2"), 7: ("Q3", "V")}
        TURN_LATE = {3: (8,), 4: (11,), 5: (12,), 6: (13,), 7: (14, 15)}

        def turn_job(name):
            return TURN.index(name) + jbase(0) + PER_J * (NKV - 1) + 6

        def ln_job(L):
            if L < 4:
                return L
            if L < 8:
                return 6 + L
            if L < 16:
                return TURN.index(L) + jbase(0) + PER_J * (NKV - 1) + 6
            if L < 20:
                return FFN_JOB + 12 + L - 16
            return FFN_JOB + 16 + L - 20

        def ln_src(L):
            if L < 16:
                return xin[:, xpos[("ln", L)] % 2, :]
            return x1_tile(L - 16)

        def x1_tile(t):
            if t < 4:
                return x1a[:, t, :]
            if t < 8:
                return x1b[:, t - 4, :]
            return y[:, t - 8, :]

        def ln_dst(L, part):
            if L < 16:
                return hT[:, part, :, (L % 8) * P:(L % 8 + 1) * P]
            i = L - 16
            return qT[(i // 4) % 2][:, part, :, (i % 4) * P:(i % 4 + 1) * P]

        def weight_pieces(u):
            if u == 2:
                return [(6 + h, (wos[:, 0, h], wos[:, 1, h])) for h in range(G)]
            slots = {3: (0, 1, 2), 4: (3, 4), 5: (5,)}[u]
            return [(10 + i, (wp[:, 0, i, :], wp[:, 1, i, :])) for i in slots]

        @block.tensor
        def _(pe):
            def mm3(o, hi_l, lo_l, hi_r, lo_r, start, stop):
                nc.tensor.matmul(o, hi_l, hi_r, start=start, stop=False, skip_group_check=True)
                nc.tensor.matmul(o, hi_l, lo_r, start=False, stop=False, skip_group_check=True)
                return nc.tensor.matmul(o, lo_l, hi_r, start=False, stop=stop, skip_group_check=True)

            def trans(f, u):
                f.wait(u_norm, PER_U, u + 1)
                f.wait(u_phi, PER_U, u)
                f.wait(u_plo, PER_U, u)
                for h in range(G):
                    last = nc.tensor.transpose(pTr[:, h * P:(h + 1) * P], pr[:, u % 2, h, :], ident[:])
                last.then_inc(u_trans, 1)

            def scores(f, u, b):
                t = u % NT
                if b == 1 and u == 0:
                    pe.wait_ge(j_done, turn_job("Q3") + 1)
                else:
                    f.wait(j_done, PER_J, jbase(b) - 1 + (6 if t >= CH else 0) + PER_J * (u // NT))
                f.wait(u_merge, PER_U, u)
                q = qT[t // CH]
                qs = slice((t % CH) * P, (t % CH + 1) * P)
                lo = 0 if t else P
                ks = slice(t * P - P + lo, t * P + P)
                for h in range(G):
                    last = mm3(pS[:, h * 256 + lo:(h + 1) * 256], q[:, 0, h, qs], q[:, 1, h, qs],
                               kv[:, 0, 0, ks], kv[:, 1, 0, ks], True, True)
                last.then_inc(u_scores, 1)

            def p_times_v(f, u, b):
                t = u % NT
                f.wait(u_mask, PER_U, u + 1)
                f.wait(j_done, PER_J, jbase(b) + (6 if t >= CH else 0) + PER_J * (u // NT))
                for own in ((1, 0) if t else (0,)):
                    tt = t - own
                    v_hi, v_lo = (kv[:, i, 1, tt * P:(tt + 1) * P] for i in range(2))
                    last = mm3(pAv[:], v_hi, v_lo, pm[:, own, 0].rearrange("p h q -> p (h q)"),
                               pm[:, own, 1].rearrange("p h q -> p (h q)"), own == 1 or t == 0, own == 0)
                last.then_inc(u_av, 1)

            def out_proj(f, u):
                f.wait(u_olo, PER_U, u + 1)
                f.wait(w_lo, PER_W, 10 * (u // NT) + 10)
                f.wait(u_y, PER_U, u + 1)
                for h in range(G):
                    last = mm3(pOp[:], oT[:, 0, h], oT[:, 1, h], wos[:, 0, h], wos[:, 1, h], h == 0, h == G - 1)
                last.then_inc(u_op, 1)

            def bank_free(f, per, j, r=None):
                f.wait(j_act, per, j - 1)
                if r is None:
                    f.wait(j_done, per, j - 1)
                elif r:
                    f.wait(r_cos, PER_R, r)

            def project(f, name, ch, j, w, r=None):
                bank_free(f, PER_J, j, r)
                f.wait(w_lo, PER_W, w)
                i = SLOT[name]
                o = pP[j % 2]
                for k in range(KT):
                    last = mm3(o[:], wp[:, 0, i, k * P:(k + 1) * P], wp[:, 1, i, k * P:(k + 1) * P],
                               hT[:, 0, k, ch * CT:(ch + 1) * CT], hT[:, 1, k, ch * CT:(ch + 1) * CT],
                               k == 0, k == KT - 1)
                last.then_inc(j_pe, 1)

            def turn_rope(name):
                before = (["Q3", "V"] + TURN)[TURN.index(name)]
                if before in SLOT and before != "V":
                    return PER_R * (NKV - 1) + (10 if before in TURN[:TURN.index(name)] else 5) + SLOT[before] + 1
                return 0

            def turn_v(f, j):
                f.wait(j_act, PER_J, j + 1)
                f.wait(j_done, PER_J, j - 5)
                for t in range(CH):
                    last = nc.tensor.transpose(pXx[:, t * P:(t + 1) * P], rB[:, j % 3, t * P:(t + 1) * P], ident[:])
                last.then_inc(v_turn, 1)

            def ln_transpose(L):
                j = ln_job(L)
                r = 0
                if L == 4:
                    r = SLOT["Q3"] + 1
                if 8 < L < 16:
                    r = turn_rope(L)
                if L in (8, 16, 17):
                    r = None
                bank_free(Frame(pe, 0), 0, j, r)
                pe.wait_ge(l_norm, L + 1)
                for k in range(KT):
                    last = nc.tensor.transpose(pP[j % 2][:, k * P:(k + 1) * P], xh[:, L % 2, k * P:(k + 1) * P],
                                               ident[:])
                last.then_inc(j_pe, 1)

            def weight_transpose(i):
                j = FFN_JOB + i
                W = 10 * STEPS + i
                bank_free(Frame(pe, 0), 0, j)
                pe.wait_ge(w_in[W % 5], 16 * (W // 5 + 1))
                for k in range(KT):
                    last = nc.tensor.transpose(pP[j % 2][:, k * P:(k + 1) * P], st[:, W % 5, k * P:(k + 1) * P],
                                               ident[:])
                last.then_inc(j_pe, 1)

            def filler(i):
                if i < 12:
                    weight_transpose(i)
                else:
                    ln_transpose(4 + i)

            def slot_jobs(f, u, b):
                js, second = u // NT, u % NT >= CH
                for name in JOBS_OF_U[u % CH]:
                    project(f, name, 0 if second else 1,
                            jbase(b) + (6 if second else 0) + PER_J * js + SLOT[name],
                            10 * (js + second) + SLOT[name] + 1,
                            PER_R * js + (10 if second else 5) + SLOT[name] - 1 if SLOT[name] >= 2 else None)

            def slot_late(f, u, b):
                js, second = u // NT, u % NT >= CH
                if u % CH == 3:
                    turn_v(f, jbase(b) + (6 if second else 0) + PER_J * js + SLOT["V"])

            def unit_step(f, u, b, jobs, late=lambda: None, prev=True, prev2=True):
                scores(f, u, b)
                if prev2:
                    p_times_v(f, u - 2, b if u >= 2 else b - 1)
                if prev:
                    trans(f, u - 1)
                jobs()
                if prev2:
                    out_proj(f, u - 2)
                late()

            def mod_row(r):
                w = ROW_BLOCK[r]
                pe.wait_ge(s_wm[w], 16)
                if r == 5:
                    pe.wait_ge(s_gdve, 3)
                for k in range(KT):
                    last = nc.tensor.matmul(row_banks[r], csil[:, k, :], wm[w][:, k, :],
                                            start=(k == 0), stop=(k == KT - 1))
                last.then_inc(s_row, 1)

            def mod_columns(kind, copied):
                for i in range(2):
                    pe.wait_ge(s_rowc, copied + i)
                    for k in range(KT):
                        at = 8 * (kind + i) + 2 * k
                        last = nc.tensor.transpose(pXx[:, at:at + B], crow[:, i, k * P:(k + 1) * P], ident[0:B, 0:B])
                last.then_inc(s_mod, 1)

            pe.wait_ge(s_const, 4)
            pe.wait_ge(s_c, 16)
            nc.tensor.transpose(pXx[:, 0:B * KT], c8[:], ident[0:B * KT, 0:B * KT]).then_inc(s_cT, 1)
            pe.wait_ge(s_cdve, 3)
            mod_row(0)
            ln_transpose(0)
            ln_transpose(1)
            mod_row(1)
            mod_columns(0, 1)
            ln_transpose(2)
            ln_transpose(3)
            mod_row(2)
            pe.wait_ge(j_done, 4)
            f0 = Frame(pe, 0)
            for name in SLOT:
                project(f0, name, 0, 4 + SLOT[name], SLOT[name] + 1, SLOT[name] - 1 if SLOT[name] >= 2 else None)
            mod_row(3)
            turn_v(f0, 9)
            ln_transpose(4)
            ln_transpose(5)
            mod_row(4)
            ln_transpose(6)
            mod_row(5)
            ln_transpose(7)

            def gates(pair):
                for i in (2 * pair, 2 * pair + 1):
                    if i == 0:
                        pe.wait_ge(s_gdve, 7)
                    if i == 2:
                        pe.wait_ge(s_modT, 2)
                    if i == 3:
                        pe.wait_ge(s_bc, 1)
                    nc.tensor.matmul(gate_banks[i], sel[:, i % 2, :], grow[:, i // 2, :], start=True, stop=True
                                     ).then_inc(s_gate, 1)

            regs = loop_registers(pe, "pe", (PER_J, PER_U, PER_W))
            for b in range(B):
                s0 = b * NKV
                f = Frame(pe, s0)

                def first_jobs(u):
                    if b == 0:
                        if u == 0:
                            pe.wait_ge(j_done, 10)
                            mod_columns(2, 3)
                        gates(u)
                    if u == 0:
                        pe.wait_ge(j_done, ln_job(8 * b + 7) + 1)
                    slot_jobs(f, u, b)
                for u in range(2):
                    unit_step(f, u, b, lambda: first_jobs(u), prev=b > 0 or u > 0, prev2=b > 0)
                if b == 0:
                    pe.wait_ge(s_bc, 4)
                with nc.tensor.Fori(s0, s0 + NKV - 1) as s:
                    f = Frame(pe, s, regs, s0)
                    for u in range(2, NT + 2):
                        unit_step(f, u, b, lambda: slot_jobs(f, u, b), lambda: slot_late(f, u, b))
                f = Frame(pe, s0 + NKV - 1)
                for u in range(2, CH):
                    def late():
                        slot_late(f, u, b)
                        if b == 0 and u == 3:
                            ln_transpose(8)
                    unit_step(f, u, b, lambda: slot_jobs(f, u, b), late)
                for u in range(CH, NT):
                    def jobs():
                        if b == 0:
                            for name in TURN_NOW[u]:
                                if name in (9, 10):
                                    ln_transpose(name)
                                    continue
                                if name == "K":
                                    pe.wait_ge(j_done, ln_job(11) + 1)
                                j = turn_job(name)
                                project(Frame(pe, 0), name, 0, j, PER_W * (NKV - 1) + 10 + SLOT[name] + 1,
                                        turn_rope(name))
                        else:
                            for i in (0, 1):
                                filler(4 * (u - 4) + i)

                    def late():
                        if b == 1:
                            for i in (2, 3):
                                filler(4 * (u - 4) + i)
                        if b == 0:
                            if u == 7:
                                turn_v(Frame(pe, 0), turn_job("V"))
                            for L in TURN_LATE[u]:
                                ln_transpose(L)
                    unit_step(f, u, b, jobs, late)

            def ff_up(i, between=lambda: None):
                c, mp = i // 4, i % 4
                if mp == 0:
                    pe.wait_ge(j_done, ln_job(16 + 4 * c + 3) + 1)
                if i >= 2:
                    pe.wait_ge(f_silu, i - 1)
                    pe.wait_ge(f_x4, i - 1)
                banks = [pS[:, 0:512], pS[:, 512:1024]] if i % 2 == 0 else [pTr[:], pAv[:]]
                q = qT[c % 2]
                for part in range(2):
                    m = mp + 4 * part
                    for k in range(KT):
                        last = mm3(banks[part], hT[:, 0, k, m * P:(m + 1) * P], hT[:, 1, k, m * P:(m + 1) * P],
                                   q[:, 0, k, :], q[:, 1, k, :], k == 0, k == KT - 1)
                    if part == 0:
                        between()
                last.then_inc(f_pe, 1)

            def x4_of(c):
                return wos if c % 2 == 0 else kv[:].rearrange("p i a (m t) -> p i (a m) t", m=2)

            def ff_down(i):
                c, t = i // 4, i % 4
                pe.wait_ge(f_lo, 4 * c + 4)
                if i >= 2:
                    pe.wait_ge(f_gated, i - 1)
                o = [pOp, pXx][i % 2]
                x4 = x4_of(c)
                for m in range(4):
                    last = mm3(o[:], x4[:, 0, m, t * P:(t + 1) * P], x4[:, 1, m, t * P:(t + 1) * P],
                               wp[:, 0, m, :], wp[:, 1, m, :], m == 0, m == 3)
                last.then_inc(f_out, 1)

            fl = Frame(pe, STEPS)
            pe.wait_ge(j_done, FFN_JOB + 12)
            p_times_v(fl, -2, 1)
            trans(fl, -1)
            pe.wait_ge(u_merge, PER_U * STEPS)
            out_proj(fl, -2)
            ff_up(0)
            p_times_v(fl, -1, 1)

            def last_unit():
                out_proj(fl, -1)
                pe.wait_ge(u_y, PER_U * STEPS + 1)

            pe.wait_ge(u_plo, PER_U * STEPS)
            ff_up(1, last_unit)
            ln_transpose(20)
            ln_transpose(21)
            ff_up(2)
            ln_transpose(22)
            ln_transpose(23)
            ff_up(3)
            for i in range(4, 16):
                if i < 12:
                    ln_transpose(20 + i)
                ff_up(i)
                ff_down(i - 4)
            for i in range(12, 16):
                ff_down(i)

        @block.scalar
        def _(act):
            def split_weight(f, dst, W, slot):
                f.wait(w_in[slot], 32, 16 * (W // 5 + 1))
                nc.scalar.copy(dst, st[:, slot, :]).then_inc(w_hi, 1)

            def result_hi(f, u):
                f.wait(u_av, PER_U, u + 1)
                nc.scalar.copy(oT[:, 0].rearrange("p h q -> p (h q)"), pAv[:]).then_inc(u_ohi, 1)

            def p_hi(f, u):
                f.wait(u_trans, PER_U, u + 1)
                f.wait(u_mask, PER_U, u)
                nc.scalar.copy(pT[:, 0].rearrange("p h q -> p (h q)"), pTr[:]).then_inc(u_phi, 1)

            def own_tile(f, u):
                f.wait(u_scores, PER_U, u + 1)
                f.wait(u_trans, PER_U, u - 1)
                nc.scalar.copy(pr[:, u % 2], pS[:].rearrange("p (h a k) -> p h a k", h=G, a=2)[:, :, 1, :]
                               ).then_inc(u_own, 1)

            def exps(f, u):
                f.wait(u_nbias, PER_U, u + 1)
                f.wait(u_norm, PER_U, u - 1)
                for h in range(G):
                    last = nc.scalar.activation(pr[:, u % 2, h, :], pr[:, u % 2, h, :], ACT.Exp,
                                                bias=nb[:, u % 2, h:h + 1], scale=SCALE,
                                                accum_out=sums[:, u % 2, h:h + 1])
                last.then_inc(u_exp, 1)

            def swap(f, j):
                f.wait(j_pe, PER_J, j + 1)
                f.wait(j_done, PER_J, j - 2)
                r = j % 3
                nc.scalar.copy(rB[0:64, r, :], pP[j % 2][64:128, :])
                nc.scalar.copy(rB[64:128, r, :], pP[j % 2][0:64, :]).then_inc(j_act, 1)

            def rope_hi(f, name, ch, j, r):
                f.wait(r_sum, PER_R, r)
                dst = kv[:, 0, 0, ch * CT:(ch + 1) * CT] if name == "K" else qT[ch][:, 0, SLOT[name] - 1, :]
                nc.scalar.copy(dst, rA[:, j % 3, :]).then_inc(r_hi, 1)

            def v_copy(f, j):
                f.wait(j_pe, PER_J, j + 1)
                f.wait(j_done, PER_J, j - 2)
                nc.scalar.copy(rB[:, j % 3, :], pP[j % 2][:]).then_inc(j_act, 1)

            def v_hi(f, ch, v):
                f.wait(v_turn, PER_V, v)
                nc.scalar.copy(kv[:, 0, 1, ch * CT:(ch + 1) * CT], pXx[:]).then_inc(v_half, 1)

            def jobs_act(f, u, b, js=0):
                t = u % NT
                a = t < CH
                ch = 1 if a else 0
                jb = jbase(b) + (0 if a else 6) + PER_J * js
                rb = (5 if a else 10) + PER_R * js

                def sw(n):
                    swap(f, jb + SLOT[n])

                def hi(n):
                    rope_hi(f, n, ch, jb + SLOT[n], rb + SLOT[n] + 1)
                if t % CH == 0:
                    sw("K"), sw("Q0")
                elif t % CH == 1:
                    hi("K"), hi("Q0"), sw("Q1")
                elif t % CH == 2:
                    hi("Q1"), sw("Q2"), sw("Q3")
                else:
                    hi("Q2"), hi("Q3"), v_copy(f, jb + 5), v_hi(f, ch, PER_V * js + (2 if a else 3))

            def ln_act(L):
                j = ln_job(L)
                kind = 0 if L < 16 else 2
                b = (L % 16) // 8
                act.wait_ge(j_pe, j + 1)
                if j >= 3:
                    act.wait_ge(j_done, j - 2)
                for k in range(KT):
                    last = nc.scalar.activation(rA[:, j % 3, k * P:(k + 1) * P], pP[j % 2][:, k * P:(k + 1) * P],
                                                ACT.Identity, bias=modT[:, kind, k, b:b + 1],
                                                scale=modT[:, kind + 1, k, b:b + 1])
                last.then_inc(j_act, 1)
                if L < 4:
                    return
                act.wait_ge(j_act, j + 1)
                nc.scalar.copy(ln_dst(L, 0), rA[:, j % 3, :].rearrange("p (k t) -> p k t", k=KT)).then_inc(l_hi, 1)

            def weight_tr_act(i):
                j = FFN_JOB + i
                act.wait_ge(j_pe, j + 1)
                dst = hT[:, 0, :, i * P:(i + 1) * P] if i < 8 else wp[:, 0, 0:4, (i - 8) * P:(i - 7) * P]
                last = nc.scalar.copy(dst, pP[j % 2][:].rearrange("p (k t) -> p k t", k=KT))
                last.then_inc(j_act, 1)

            def filler(i):
                if i < 12:
                    weight_tr_act(i)
                else:
                    if i == 12:
                        act.wait_ge(s_modT, 2)
                    ln_act(4 + i)

            def splits(f, u, b):
                for k, dst in weight_pieces(u):
                    if k >= 10:
                        f.wait(j_pe, PER_J, jbase(b) + k - 10 + 1)
                    split_weight(f, dst[0], k, k % 5)

            def unit_step(f, u, b, jobs, prev=True, prev2=True, split=True):
                own_tile(f, u)
                if u == 2:
                    splits(f, u, b)
                if prev2:
                    result_hi(f, u - 2)
                if prev:
                    p_hi(f, u - 1)
                exps(f, u)
                jobs()
                if split and u in (3, 4, 5):
                    splits(f, u, b)

            act.dma_start(c8[:], cond.rearrange("b (k p) -> (b k) p", p=P)).then_inc(s_c, 16)
            for i in (0, 1):
                act.dma_start(wm[i][:], wmod[:, i * D:(i + 1) * D].rearrange("(k p) n -> p k n", p=P)
                              ).then_inc(s_wm[i], 16)
            act.wait_ge(s_cT, 1)
            nc.scalar.activation(cT[:, 0].rearrange("p b k -> p (b k)"), pXx[:, 0:B * KT], ACT.Exp, scale=-1.0
                                 ).then_inc(s_cact, 1)

            def row_copy(r, slot):
                act.wait_ge(s_row, r + 1)
                nc.scalar.copy(crow[:, slot, :], row_banks[r]).then_inc(s_rowc, 1)

            def gate_copies(pair):
                for i in (2 * pair, 2 * pair + 1):
                    act.wait_ge(s_gate, i + 1)
                    nc.scalar.copy(bc[:, i // 2, i % 2, :], gate_banks[i]).then_inc(s_bc, 1)

            f0 = Frame(act, 0)
            row_copy(0, 0)
            row_copy(1, 1)
            split_weight(f0, wp[:, 0, 0, :], 0, 0)
            act.wait_ge(s_modT, 1)
            for L in range(4):
                ln_act(L)
            for k in range(1, 6):
                split_weight(f0, wp[:, 0, k, :], k, k % 5)
            for name in SLOT:
                j = 4 + SLOT[name]
                if name != "V":
                    swap(f0, j)
                if name not in ("K",):
                    prev_name = list(SLOT)[SLOT[name] - 1]
                    rope_hi(f0, prev_name, 0, j - 1, SLOT[prev_name] + 1)
                if name == "V":
                    v_copy(f0, j)
                    v_hi(f0, 0, 1)
            for L in range(4, 7):
                ln_act(L)
            act.wait_ge(s_mod, 1)
            row_copy(4, 0)
            ln_act(7)
            row_copy(5, 1)

            regs = loop_registers(act, "act", (PER_J, PER_U, PER_W, PER_V, 32))
            for b in range(B):
                s0 = b * NKV
                f = Frame(act, s0)

                def first_jobs(u):
                    if b == 0:
                        gate_copies(u)
                    jobs_act(f, u, b)
                for u in range(2):
                    unit_step(f, u, b, lambda: first_jobs(u), prev=s0 > 0 or u > 0, prev2=s0 > 0)
                with nc.scalar.Fori(s0, s0 + NKV - 1) as s:
                    f = Frame(act, s, regs, s0)
                    for u in range(2, NT + 2):
                        unit_step(f, u, b, lambda: jobs_act(f, u, b, js=u // NT))
                f = Frame(act, s0 + NKV - 1)
                for u in range(2, NT):
                    def jobs():
                        if u < CH:
                            jobs_act(f, u, b)
                        elif b == 0:
                            fz, r7 = Frame(act, 0), PER_R * (NKV - 1) + 10
                            if u == 4:
                                ln_act(9), ln_act(10)
                            for name in TURN_NOW[u]:
                                if name in SLOT and name != "V":
                                    swap(fz, turn_job(name))
                                if name == "V":
                                    v_copy(fz, turn_job("V"))
                            for name in TURN_NOW[u]:
                                if name in SLOT and name not in ("Q3", "V"):
                                    rope_hi(fz, name, 0, turn_job(name), r7 + SLOT[name] + 1)
                        else:
                            filler(4 * (u - 4)), filler(4 * (u - 4) + 1)
                    unit_step(f, u, b, jobs, split=b == 0)
                    if b == 0 and u >= 3:
                        if u == 7:
                            v_hi(Frame(act, 0), 0, PER_V * (NKV - 1) + 3)
                            ln_act(14)
                            rope_hi(Frame(act, 0), "Q3", 0, turn_job("Q3"), PER_R * (NKV - 1) + 10 + SLOT["Q3"] + 1)
                            ln_act(15)
                        else:
                            for L in TURN_LATE[u]:
                                ln_act(L)
                    if b == 1 and u >= CH:
                        filler(4 * (u - 4) + 2)
                        if u < 7:
                            filler(4 * (u - 4) + 3)

            fl = Frame(act, STEPS)
            result_hi(fl, -2)
            p_hi(fl, -1)
            filler(15)
            result_hi(fl, -1)

            def ff_act(i):
                c, mp = i // 4, i % 4
                act.wait_ge(f_pe, i + 1)
                if i >= 2:
                    act.wait_ge(f_x4, i - 1)
                bank = pS[:, 0:512] if i % 2 == 0 else pTr[:]
                nc.scalar.activation(pr[:, i % 2].rearrange("p h q -> p (h q)"), bank, ACT.Silu,
                                     bias=b12T[:, mp:mp + 1]).then_inc(f_silu, 1)
                act.wait_ge(f_x4, i + 1)
                if c >= 2 and mp == 0:
                    act.wait_ge(f_out, 4 * (c - 1))
                if c == 0 and mp == 0:
                    act.wait_ge(u_op, PER_U * STEPS)
                x4 = wos if c % 2 == 0 else kv[:].rearrange("p i a (m t) -> p i (a m) t", m=2)
                nc.scalar.copy(x4[:, 0, mp, :], rB[:, i % 3, :]).then_inc(f_hi, 1)

            for i in range(16):
                for L in {2: (20, 21), 3: (22, 23)}.get(i, (20 + i,) if 4 <= i < 12 else ()):
                    ln_act(L)
                ff_act(i)

        @block.vector
        def _(dve):
            def result_lo(f, u):
                f.wait(u_ohi, PER_U, u + 1)
                nc.vector.tensor_tensor(oT[:, 1].rearrange("p h q -> p (h q)"), pAv[:],
                                        oT[:, 0].rearrange("p h q -> p (h q)"), ALU.subtract).then_inc(u_olo, 1)

            def p_lo(f, u):
                f.wait(u_phi, PER_U, u + 1)
                nc.vector.tensor_tensor(pT[:, 1].rearrange("p h q -> p (h q)"), pTr[:],
                                        pT[:, 0].rearrange("p h q -> p (h q)"), ALU.subtract).then_inc(u_plo, 1)

            def merge(f, u):
                f.wait(u_own, PER_U, u + 1)
                f.stand()
                before = pS[:].rearrange("p (h a k) -> p h a k", h=G, a=2)[:, :, 0, :]
                if u % NT == 0:
                    before = lowest[:].unsqueeze(1).to_broadcast([P, G, P])
                nc.vector.copy_predicated(pr[:, u % 2], older[:].unsqueeze(1).to_broadcast([P, G, P]), before
                                          ).then_inc(u_merge, 1)
                f.wait(u_merge, PER_U, u + 1)
                nc.vector.tensor_reduce(mx[:, u % 2, :], pr[:, u % 2], AX.X, ALU.max, negate=True
                                        ).then_inc(u_max, 1)
                f.wait(u_max, PER_U, u + 1)
                nc.vector.tensor_scalar(nb[:, u % 2, :], mx[:, u % 2, :], SCALE, None, ALU.mult
                                        ).then_inc(u_nbias, 1)

            def recip(f, u):
                f.wait(u_exp, PER_U, u + 1)
                nc.vector.reciprocal(rs[:, u % 2, :], sums[:, u % 2, :]).then_inc(u_rsum, 1)

            def rope_cos(f, ch, j):
                f.wait(j_act, PER_J, j + 1)
                f.wait(j_done, PER_J, j - 2)
                nc.vector.tensor_tensor(rA[:, j % 3, :], pP[j % 2][:], tab[:, 0, ch * CT:(ch + 1) * CT],
                                        ALU.mult).then_inc(r_cos, 1)

            def rope_sum(f, j, r):
                f.wait(r_sin, PER_R, r)
                f.wait(r_cos, PER_R, r)
                nc.vector.tensor_tensor(rA[:, j % 3, :], rA[:, j % 3, :], rB[:, j % 3, :], ALU.add
                                        ).then_inc(r_sum, 1)

            def rope_lo(f, name, ch, j, r):
                f.wait(r_hi, PER_R, r)
                dst, hi = ((kv[:, i, 0, ch * CT:(ch + 1) * CT] if name == "K" else qT[ch][:, i, SLOT[name] - 1, :])
                           for i in (1, 0))
                nc.vector.tensor_tensor(dst, rA[:, j % 3, :], hi, ALU.subtract).then_inc(j_done, 1)

            def v_lo(f, ch, v):
                f.wait(v_half, PER_V, v)
                nc.vector.tensor_tensor(kv[:, 1, 1, ch * CT:(ch + 1) * CT], pXx[:],
                                        kv[:, 0, 1, ch * CT:(ch + 1) * CT], ALU.subtract).then_inc(j_done, 1)

            def add_y(f, u, b):
                t = u % NT
                f.wait(u_op, PER_U, u + 1)
                dve.wait_ge(s_zero, 1 + (NT if b else 0))
                nc.vector.tensor_tensor(y[:, t, :], y[:, t, :], pOp[:], ALU.add).then_inc(u_y, 1)

            def jobs_dve(f, u, b, mid, js=0):
                t = u % NT
                a = t < CH
                ch = 1 if a else 0
                jb = jbase(b) + (0 if a else 6) + PER_J * js
                rb = (5 if a else 10) + PER_R * js

                def cos_(n):
                    rope_cos(f, ch, jb + SLOT[n])

                def sum_(n):
                    rope_sum(f, jb + SLOT[n], rb + SLOT[n] + 1)

                def lo(n):
                    rope_lo(f, n, ch, jb + SLOT[n], rb + SLOT[n] + 1)
                if t % CH == 0:
                    mid(), cos_("K"), cos_("Q0")
                elif t % CH == 1:
                    sum_("K"), sum_("Q0"), mid(), lo("K"), lo("Q0"), cos_("Q1")
                elif t % CH == 2:
                    sum_("Q1"), mid(), lo("Q1"), cos_("Q2"), cos_("Q3")
                else:
                    sum_("Q2"), sum_("Q3"), mid(), lo("Q2"), lo("Q3")

            def late_dve(f, u, js=0):
                if u % CH == 3:
                    a = u % NT < CH
                    v_lo(f, 1 if a else 0, PER_V * js + (2 if a else 3))

            def ln_stats(L):
                if L < 16:
                    x_arrived(dve, ("ln", L))
                if L >= 24:
                    dve.wait_ge(s_fin, L - 16 + 1)
                if L in (16, 20):
                    dve.wait_ge(x1_in[L // 4 - 4], 16)
                nc.vector.bn_stats(stat[:, L % 2, :], ln_src(L)).then_inc(l_stat, 1)
                dve.wait_ge(l_stat, 2 * L + 1)
                nc.vector.bn_aggr(mv[:, L % 2, 0:2], stat[:, L % 2, :]).then_inc(l_stat, 1)
                dve.wait_ge(l_stat, 2 * L + 2)
                nc.vector.tensor_scalar(mv[:, L % 2, 2:3], mv[:, L % 2, 1:2], EPS, None, ALU.add
                                        ).then_inc(l_var, 1)

            def ln_apply(L):
                dve.wait_ge(l_rstd, L + 1)
                if L >= 2:
                    dve.wait_ge(j_pe, ln_job(L - 2) + 1)
                nc.vector.tensor_scalar(xh[:, L % 2, :], ln_src(L), mv[:, L % 2, 0:1], mv[:, L % 2, 3:4],
                                        ALU.subtract, ALU.mult).then_inc(l_norm, 1)

            def ln_norm(L):
                ln_stats(L)
                ln_apply(L)

            def ln_lo(L):
                j = ln_job(L)
                if L < 4:
                    dve.wait_ge(j_act, j + 1)
                    nc.vector.tensor_copy(ln_dst(L, 0), rA[:, j % 3, :].rearrange("p (k t) -> p k t", k=KT)
                                          ).then_inc(l_hi, 1)
                dve.wait_ge(l_hi, L + 1)
                nc.vector.tensor_tensor(ln_dst(L, 1), rA[:, j % 3, :].rearrange("p (k t) -> p k t", k=KT),
                                        ln_dst(L, 0), ALU.subtract).then_inc(j_done, 1)

            def weight_tr_lo(i):
                j = FFN_JOB + i
                dve.wait_ge(j_act, j + 1)
                dst, hi = ((hT[:, a, :, i * P:(i + 1) * P] if i < 8 else wp[:, a, 0:4, (i - 8) * P:(i - 7) * P])
                           for a in (1, 0))
                nc.vector.tensor_tensor(dst, pP[j % 2][:].rearrange("p (k t) -> p k t", k=KT), hi, ALU.subtract
                                        ).then_inc(j_done, 1)

            def filler(i):
                if i < 12:
                    weight_tr_lo(i)
                else:
                    ln_lo(4 + i)

            def split_weight(f, dst, W, slot):
                f.wait(w_hi, PER_W, W + 1)
                nc.vector.tensor_tensor(dst[1], st[:, slot, :], dst[0], ALU.subtract).then_inc(w_lo, 1)

            def splits(f, u):
                for k, dst in weight_pieces(u):
                    split_weight(f, dst, k, k % 5)

            def unit_step(f, u, b, jobs, late=lambda: None, prev=True, prev2=True, split=True):
                merge(f, u)
                if u == 2:
                    splits(f, u)
                if prev2:
                    result_lo(f, u - 2)
                if prev:
                    p_lo(f, u - 1)
                jobs(lambda: recip(f, u))
                if split and u in (3, 4, 5):
                    splits(f, u)
                if prev2:
                    b2 = b if u >= 2 else b - 1
                    add_y(f, u - 2, b2)
                late()

            dve.wait_ge(s_cact, 1)
            nc.vector.tensor_scalar(cT[:, 0], cT[:, 0], 1.0, None, ALU.add).then_inc(s_cdve, 1)
            dve.wait_ge(s_cdve, 1)
            nc.vector.reciprocal(cT[:, 1], cT[:, 0]).then_inc(s_cdve, 1)
            dve.wait_ge(s_cdve, 2)
            nc.vector.tensor_tensor(csil[:].rearrange("p k b -> p b k"),
                                    pXx[:, 0:B * KT].rearrange("p (b k) -> p b k", b=B), cT[:, 1], ALU.mult
                                    ).then_inc(s_cdve, 1)
            nc.vector.tensor_copy(older[:], rA[:, 2, 0:P]).then_inc(s_cdve, 1)

            f0 = Frame(dve, 0)
            for L in range(4):
                ln_norm(L)

            def mod_out(kind):
                nc.vector.tensor_copy(modT[:, kind], pXx[:, 8 * kind:8 * kind + 8].rearrange(
                    "p (k b) -> p k b", k=KT))
                return nc.vector.tensor_scalar(modT[:, kind + 1], pXx[:, 8 * kind + 8:8 * kind + 16].rearrange(
                    "p (k b) -> p k b", k=KT), 1.0, None, ALU.add)

            dve.wait_ge(s_mod, 1)
            mod_out(0).then_inc(s_modT, 1)
            split_weight(f0, (wp[:, 0, 0, :], wp[:, 1, 0, :]), 0, 0)
            for L in range(4):
                ln_lo(L)
            for k in range(1, 6):
                split_weight(f0, (wp[:, 0, k, :], wp[:, 1, k, :]), k, k % 5)

            def gate_row(gate):
                bank, g = row_banks[2 + gate], grow[:, gate, :]
                dve.wait_ge(s_row, gate + 3)
                nc.vector.tensor_scalar(g, bank, 0.0, 0.5, ALU.is_ge, ALU.subtract).then_inc(s_gdve, 1)
                dve.wait_ge(s_gdve, 3 * gate + 1)
                nc.vector.scalar_tensor_tensor(out=gmag[:], in0=g, scalar=4.0, in1=bank, op0=ALU.mult,
                                               op1=ALU.mult).then_inc(s_gdve, 1)
                dve.wait_ge(s_gdve, 3 * gate + 2)
                nc.vector.scalar_tensor_tensor(out=g, in0=gmag[:], scalar=2 * MIN_GATE, in1=g, op0=ALU.max,
                                               op1=ALU.mult).then_inc(s_gdve, 1)

            gate_row(0)
            dve.wait_ge(s_tab, 32)
            names = list(SLOT)
            for i in range(5):
                rope_cos(f0, 0, 4 + i)
                if i:
                    rope_lo(f0, names[i - 1], 0, 3 + i, i)
                rope_sum(f0, 4 + i, i + 1)
                if i in (2, 3):
                    ln_apply(2 + i)
                if i in (1, 2):
                    ln_stats(3 + i)
            rope_lo(f0, "Q3", 0, 8, 5)
            v_lo(f0, 0, 1)
            ln_stats(6), ln_lo(4), ln_apply(6), ln_stats(7), gate_row(1), ln_lo(5), ln_apply(7), ln_lo(6), ln_lo(7)
            nc.vector.tensor_copy(sel[:], ident[0:B, 0:B].unsqueeze(2).to_broadcast([B, B, P])).then_inc(s_gdve, 1)

            regs = loop_registers(dve, "dve", (PER_J, PER_U, PER_W, PER_V))
            for b in range(B):
                s0 = b * NKV
                f = Frame(dve, s0)

                def first_jobs(u, mid):
                    if (b, u) == (0, 0):
                        dve.wait_ge(s_mod, 2)
                        mod_out(2).then_inc(s_modT, 1)
                    jobs_dve(f, u, b, mid)
                for u in range(2):
                    unit_step(f, u, b, lambda mid: first_jobs(u, mid), prev=s0 > 0 or u > 0, prev2=s0 > 0)
                if b == 0:
                    dve.wait_ge(s_bc, 4)
                    dve.wait_ge(s_b3, 48)
                    for i in range(B):
                        nc.vector.tensor_tensor(bc[:, 2, i, :], bc[:, 2, i, :], bc[:, 1, i, :], ALU.mult
                                                ).then_inc(s_bc, 1)
                with nc.vector.Fori(s0, s0 + NKV - 1) as s:
                    f = Frame(dve, s, regs, s0)
                    for u in range(2, NT + 2):
                        unit_step(f, u, b, lambda mid: jobs_dve(f, u, b, mid, js=u // NT),
                                  lambda: late_dve(f, u, u // NT))
                f = Frame(dve, s0 + NKV - 1)
                for u in range(2, NT):
                    def jobs(mid):
                        if u < CH:
                            if b == 0 and u == 3:
                                ln_stats(9)
                            jobs_dve(f, u, b, mid)
                            if b == 0 and u == 3:
                                ln_apply(9)
                        elif b == 0:
                            fz, r7 = Frame(dve, 0), PER_R * (NKV - 1) + 10
                            names = [n for n in TURN_NOW[u] if n in SLOT and n != "V"]
                            if u == 4:
                                ln_stats(11)
                            if u > 4:
                                ln_stats(8 + u)
                            mid()
                            if u == 4:
                                ln_lo(9), ln_apply(11), ln_lo(10)
                            for name in names:
                                rope_cos(fz, 0, turn_job(name))
                            if u == 7:
                                ln_apply(15)
                            for name in names:
                                rope_sum(fz, turn_job(name), r7 + SLOT[name] + 1)
                            for name in names:
                                rope_lo(fz, name, 0, turn_job(name), r7 + SLOT[name] + 1)
                        else:
                            if u == 7:
                                ln_stats(18), ln_stats(19)
                            mid()
                            filler(4 * (u - 4))
                            if u == 7:
                                ln_apply(18)
                            filler(4 * (u - 4) + 1)
                            if u == 7:
                                ln_apply(19)

                    def late():
                        if u < CH:
                            if b == 0 and u == 3:
                                ln_stats(10)
                            late_dve(f, u)
                            if b == 0 and u == 2:
                                ln_norm(8)
                            if b == 0 and u == 3:
                                ln_lo(8), ln_apply(10)
                        elif b == 0:
                            if u == 7:
                                v_lo(Frame(dve, 0), 0, PER_V * (NKV - 1) + 3)
                            if u == 4:
                                ln_stats(12)
                            for L in TURN_LATE[u]:
                                ln_lo(L)
                            if u < 7:
                                ln_apply(8 + u)
                        elif b == 1:
                            filler(4 * (u - 4) + 2)
                            if u < 7:
                                filler(4 * (u - 4) + 3)
                            if u == 6:
                                ln_stats(16), ln_stats(17), ln_apply(16), ln_apply(17)
                    unit_step(f, u, b, jobs, late, split=b == 0)

            fl = Frame(dve, STEPS)
            result_lo(fl, -2)
            p_lo(fl, -1)
            filler(15)
            add_y(fl, -2, 1)
            result_lo(fl, -1)
            add_y(fl, -1, 1)

            def ff_x4(i):
                mp = i % 4
                dve.wait_ge(f_silu, i + 1)
                if i >= 3:
                    dve.wait_ge(f_hi, i - 2)
                    dve.wait_ge(f_lo, i - 2)
                bank = pS[:, 512:1024] if i % 2 == 0 else pAv[:]
                nc.vector.scalar_tensor_tensor(out=rB[:, i % 3, :], in0=bank, scalar=b12T[:, 4 + mp:5 + mp],
                                               in1=pr[:, i % 2].rearrange("p h q -> p (h q)"), op0=ALU.add,
                                               op1=ALU.mult).then_inc(f_x4, 1)

            def ff_lo(i):
                c, mp = i // 4, i % 4
                dve.wait_ge(f_hi, i + 1)
                x4 = wos if c % 2 == 0 else kv[:].rearrange("p i a (m t) -> p i (a m) t", m=2)
                nc.vector.tensor_tensor(x4[:, 1, mp, :], rB[:, i % 3, :], x4[:, 0, mp, :], ALU.subtract
                                        ).then_inc(f_lo, 1)

            def ff_gate(i):
                dve.wait_ge(f_out, i + 1)
                if i >= 5:
                    dve.wait_ge(s_store[i % 5], 16 * (i // 5))
                nc.vector.tensor_tensor(st[:, i % 5, :], [pOp, pXx][i % 2][:], bc[:, 1, i // 8, :], ALU.mult
                                        ).then_inc(f_gated, 1)

            norms = {1: (20, 21), 2: (22, 23), 3: (24,), **{i: (21 + i,) for i in range(4, 11)}}
            los = {2: (20, 21), 3: (22, 23), **{i: (20 + i,) for i in range(4, 12)}}
            for i in range(16):
                for L in norms.get(i, ()):
                    ln_stats(L)
                for L in norms.get(i, ()):
                    ln_apply(L)
                for L in los.get(i, ()):
                    ln_lo(L)
                ff_x4(i)
                ff_lo(i)
                if i >= 4:
                    ff_gate(i - 4)
            for i in range(12, 16):
                ff_gate(i)

        @block.gpsimd
        def _(pool):
            def mask(f, u):
                f.wait(u_plo, PER_U, u + 1)
                f.wait(u_av, PER_U, u)
                f.stand()
                for own in ((0, 1) if u % NT else (0,)):
                    for part in range(2):
                        sign, op = (1, ALU.is_ge) if own == 0 else (-1, ALU.is_gt)
                        last = nc.gpsimd.affine_select(out=pm[:, own, part], in_=pT[:, part], compare_op=op,
                                                       fill=0.0, base=0, pattern=[[0, G], [sign, P]],
                                                       channel_multiplier=-sign)
                last.then_inc(u_mask, 1)

            def normalise(f, u):
                f.wait(u_rsum, PER_U, u + 1)
                nc.gpsimd.tensor_tensor(pr[:, u % 2], pr[:, u % 2],
                                        rs[:, u % 2, :].unsqueeze(2).to_broadcast([P, G, P]), ALU.mult
                                        ).then_inc(u_norm, 1)

            def rope_sin(f, ch, j):
                f.wait(j_act, PER_J, j + 1)
                nc.gpsimd.tensor_tensor(rB[:, j % 3, :], rB[:, j % 3, :], tab[:, 1, ch * CT:(ch + 1) * CT],
                                        ALU.mult).then_inc(r_sin, 1)

            def jobs_pool(f, u, b, js=0):
                t = u % NT
                jb = jbase(b) + (0 if t < CH else 6) + PER_J * js
                for name in JOBS_OF_U[t % CH]:
                    if name != "V":
                        rope_sin(f, 1 if t < CH else 0, jb + SLOT[name])

            def ln_rstd(L):
                pool.wait_ge(l_var, L + 1)
                nc.gpsimd.tensor_tensor(mv[:, L % 2, 3:4], mv[:, L % 2, 2:3], half[:], ALU.pow).then_inc(l_rstd, 1)

            def unit_step(f, u, b, jobs, prev=True, between=lambda: None):
                if prev:
                    mask(f, u - 1)
                between()
                normalise(f, u)
                jobs()

            def finish(f, u, b):
                t = u % NT
                f.wait(u_y, PER_U, u + 2)
                pool.wait_ge(s_bc, 2)
                nc.gpsimd.tensor_tensor(y[:, t, :], y[:, t, :], bc[:, 0, b, :], ALU.mult).then_inc(s_gated, 1)
                x_arrived(pool, ("fin", NT * b + t))
                pool.wait_ge(s_gated, NT * b + t + 1)
                nc.gpsimd.tensor_tensor(y[:, t, :], y[:, t, :], xin[:, xpos[("fin", NT * b + t)] % 2, :],
                                        ALU.add).then_inc(s_fin, 1)

            def spill(t):
                pool.wait_ge(s_fin, t + 1)
                pool.dma_start(x1_spill[t * P:(t + 1) * P, :], y[:, t, :]).then_inc(s_spill[t], 16)

            def clear_y(t):
                pool.wait_ge(s_spill[t], 16)
                pool.memset(y[:, t, :], 0.0).then_inc(s_zero, 1)

            def residual_bias(i):
                pool.wait_ge(l_norm, 16 + i + 1)
                pool.wait_ge(s_bc, 6)
                nc.gpsimd.tensor_tensor(x1_tile(i), x1_tile(i), bc[:, 2, i // NT, :], ALU.add).then_inc(f_resb, 1)

            pool.memset(ident[:], 0.0).then_inc(s_const, 1)
            pool.memset(rA[:, 2, 0:P], 1.0).then_inc(s_const, 1)
            pool.memset(lowest[:], LOWEST)
            pool.memset(half[:], -0.5)
            pool.wait_ge(s_const, 2)
            nc.gpsimd.affine_select(out=ident[:], in_=ident[:], compare_op=ALU.not_equal, fill=1.0, base=0,
                                    pattern=[[-1, P]], channel_multiplier=1).then_inc(s_const, 1)
            nc.gpsimd.affine_select(out=rA[:, 2, 0:P], in_=rA[:, 2, 0:P], compare_op=ALU.is_gt, fill=0.0, base=0,
                                    pattern=[[1, P]], channel_multiplier=-1).then_inc(s_const, 1)
            pool.wait_ge(s_const, 4)
            for L in range(4):
                ln_rstd(L)
            f0 = Frame(pool, 0)
            pool.wait_ge(s_tab, 32)
            for j in range(4, 9):
                rope_sin(f0, 0, j)
                if j in (5, 6):
                    ln_rstd(j - 1)
            ln_rstd(6)
            ln_rstd(7)
            pool.wait_ge(s_row, 4)
            pool.memset(y[:, 0:NT // 2], 0.0).then_inc(u_y, 1)
            pool.memset(y[:, NT // 2:NT], 0.0).then_inc(s_zero, 1)

            regs = loop_registers(pool, "pool", (PER_J, PER_U))
            for b in range(B):
                s0 = b * NKV
                f = Frame(pool, s0)
                for u in range(2):
                    unit_step(f, u, b, lambda: jobs_pool(f, u, b), prev=s0 > 0 or u > 0)
                    if b == 1:
                        finish(f, u - 2, 0)
                        spill(u + 5)
                        clear_y(u + 4)
                if b == 1:
                    spill(7)
                    clear_y(6)
                    clear_y(7)
                with nc.gpsimd.Fori(s0, s0 + NKV - 1) as s:
                    f = Frame(pool, s, regs, s0)
                    for u in range(2, NT + 2):
                        unit_step(f, u, b, lambda: jobs_pool(f, u, b, js=u // NT))
                f = Frame(pool, s0 + NKV - 1)
                for u in range(2, NT):
                    def jobs():
                        if u < CH:
                            jobs_pool(f, u, b)
                        elif b == 0:
                            for name in TURN_NOW[u]:
                                if name in SLOT and name not in ("Q3", "V"):
                                    rope_sin(Frame(pool, 0), 0, turn_job(name))
                        elif u == 7:
                            residual_bias(2), residual_bias(3)

                    def between():
                        for L in ({3: (9,), 4: (11,), 5: (13,), 6: (14,), 7: (15,)} if b == 0 else
                                  {7: (18, 19)}).get(u, ()):
                            ln_rstd(L)
                        if b == 0 and u == 7:
                            rope_sin(Frame(pool, 0), 0, turn_job("Q3"))
                    unit_step(f, u, b, jobs, between=between)
                    if b == 0 and u in (2, 3, 4):
                        ln_rstd(4 + 2 * u)
                    if b == 1 and u == 6:
                        ln_rstd(16), ln_rstd(17)
                    finish(f, u - 2, b)
                    if b == 1 and u == 6:
                        residual_bias(0), residual_bias(1)
                    if b == 0 and u >= 3:
                        spill(u - 3)
                    if b == 0 and u >= 4:
                        clear_y(u - 4)
            fl = Frame(pool, STEPS)
            mask(fl, -1)
            finish(fl, -2, 1)
            finish(fl, -1, 1)

            def ff_residual(i):
                pool.wait_ge(f_gated, i + 1)
                pool.wait_ge(f_resb, i + 1)
                nc.gpsimd.tensor_tensor(st[:, i % 5, :], st[:, i % 5, :], x1_tile(i), ALU.add).then_inc(f_res, 1)

            for i in range(1, 16):
                norms = {1: (20, 21), 2: (22, 23)}.get(i, (21 + i,) if 3 <= i < 11 else ())
                for L in norms:
                    ln_rstd(L)
                for L in norms:
                    residual_bias(L - 16)
                if i >= 4:
                    ff_residual(i - 4)
            for i in range(12, 16):
                ff_residual(i)

        @block.sync
        def _(sp):
            def load_piece(f, W, src):
                slot = W % 5
                f.wait(w_lo, PER_W, W - 4)
                f.stand()
                sp.dma_start(st[:, slot, :] if src.shape[-1] == 512 and len(src.shape) == 2 else
                             st[:, slot, :].rearrange("p (k n) -> p k n", k=KT), src).then_inc(w_in[slot], 16)

            def column_piece(w, col):
                return w.rearrange("(k p) n -> p k n", p=P)[:, :, bass.ds(col, DH)]

            def load_wo(f, g):
                for h in range(G):
                    load_piece(f, 6 + h, wo[bass.ds(g * (G * DH) + h * DH, DH), :])

            def load_proj(f, g, W):
                load_piece(f, W, column_piece(wk, g * DH))
                for h in range(G):
                    load_piece(f, W + 1 + h, column_piece(wq, g * (G * DH) + h * DH))
                load_piece(f, W + 5, column_piece(wv, g * DH))

            def load_x(i):
                kind, t = xseq[i]
                if i >= 2:
                    before, tb = xseq[i - 2]
                    sp.wait_ge(l_norm if before == "ln" else s_fin, tb + 1)
                sp.dma_start(xin[:, i % 2, :], x[t // NT, (t % NT) * P:(t % NT + 1) * P, :]
                             ).then_inc(x_in[i % 2], 16)

            for i in range(4):
                load_x(i)
            f0 = Frame(sp, 0)
            load_piece(f0, 0, column_piece(wk, 0))

            def load_wmod(i):
                sp.dma_start(wm[i][:], wmod[:, i * D:(i + 1) * D].rearrange("(k p) n -> p k n", p=P)
                             ).then_inc(s_wm[i], 16)
            for h in range(G):
                load_piece(f0, 1 + h, column_piece(wq, h * DH))
                if h == 1:
                    load_wmod(ROW_BLOCK[2])
            sp.dma_start(tab[:, 0, :], cos).then_inc(s_tab, 16)
            sp.dma_start(tab[:, 1, :], sin).then_inc(s_tab, 16)
            load_x(4), load_x(5)
            load_piece(f0, 5, column_piece(wv, 0))
            for i in ROW_BLOCK[3:]:
                load_wmod(i)
            for b in range(B):
                sp.dma_start(bc[:, 2, b, :], b3.rearrange("(a n) -> a n", a=1).broadcast_to([P, D])
                             ).then_inc(s_b3, 16)
            sp.dma_start(b12T[:], b12.rearrange("(m p) -> p m", p=P),
                         allow_slow_non_contiguous=True).then_inc(s_b3, 16)
            for i in range(6, 10):
                load_x(i)
            regs = loop_registers(sp, "sp", (PER_W,))
            for b in range(B):
                s0 = b * NKV
                with nc.sync.Fori(s0, s0 + NKV - 1) as s:
                    f = Frame(sp, s, regs, s0)
                    load_wo(f, s - s0)
                    load_proj(f, s - s0 + 1, 10)
                f = Frame(sp, s0 + NKV - 1)
                load_wo(f, NKV - 1)
                if b == 1:
                    load_x(24), load_x(25)
                if b == 0:
                    load_piece(f, 10, column_piece(wk, 0))
                    load_piece(f, 11, column_piece(wq, 0))
                    load_x(10)
                    for h in range(1, G):
                        load_piece(f, 11 + h, column_piece(wq, h * DH))
                    for i in range(11, 15):
                        load_x(i)
                    load_piece(f, 15, column_piece(wv, 0))
                    for i in range(15, 24):
                        load_x(i)
            for i in range(12):
                W = 10 * STEPS + i
                if W - 5 >= 10 * STEPS:
                    sp.wait_ge(j_pe, FFN_JOB + i - 5 + 1)
                else:
                    sp.wait_ge(w_lo, W - 4)
                sp.dma_start(st[:, W % 5, :], w12[i * P:(i + 1) * P, :] if i < 8 else
                             w3[(i - 8) * P:(i - 7) * P, :]).then_inc(w_in[W % 5], 16)
                for tile in {3: (10, 11), 7: (12,), 11: (13,)}.get(i, ()):
                    load_x(xpos[("fin", tile)])
                if i == 8:
                    sp.wait_ge(j_done, jbase(1) + PER_J * (STEPS - 1) + 5)
                    for t in range(4):
                        sp.wait_ge(s_spill[t], 16)
                    sp.dma_start(x1a[:], x1_spill[0:CT, :].rearrange("(t p) d -> p t d", p=P)
                                 ).then_inc(x1_in[0], 16)
            for tile in (14, 15):
                load_x(xpos[("fin", tile)])
            for t in range(4, 8):
                sp.wait_ge(s_spill[t], 16)
            sp.wait_ge(u_av, PER_U * STEPS)
            sp.dma_start(x1b[:], x1_spill[CT:2 * CT, :].rearrange("(t p) d -> p t d", p=P)).then_inc(x1_in[1], 16)
            for i in range(2 * NT):
                sp.wait_ge(f_res, i + 1)
                sp.dma_start(out[i // NT, (i % NT) * P:(i % NT + 1) * P, :], st[:, i % 5, :]
                             ).then_inc(s_store[i % 5], 16)
            for i in range(5):
                sp.wait_ge(s_store[i], 16 * ((2 * NT - i + 4) // 5))


_INS = ["L0_attn_x", "L0_attn_wq", "L0_attn_wk", "L0_attn_wv", "L0_attn_wo", "L0_ffn_w12", "L0_ffn_b12", "L0_ffn_w3",
        "L0_ffn_b3", "L0_c", "L0_wmod"]


def kernel(**inputs):
    import numpy as _np
    import concourse.bacc as _bacc
    from concourse import mybir as _mybir
    from concourse.bass_utils import run_bass_kernel_spmd as _run

    nc = _bacc.Bacc("TRN2", target_bir_lowering=False, num_devices=1)
    arrays, args = {}, []

    def take(name, a):
        arrays[name] = a
        args.append(nc.dram_tensor(name, a.shape, _mybir.dt.from_np(a.dtype), kind="ExternalInput").ap())

    for name in _INS:
        take(f"in_{name}_dram", _np.ascontiguousarray(inputs[name]))
    seq, dh = inputs["L0_attn_x"].shape[1], 128
    half = dh // 2
    freq = (10000.0 ** (-_np.arange(half) / half)).astype(_np.float32)
    angle = (freq[:, None] * _np.arange(seq, dtype=_np.float32)[None, :]).astype(_np.float64)
    take("rope_cos", _np.concatenate([_np.cos(angle), _np.cos(angle)]).astype(_np.float32))
    take("rope_sin", _np.concatenate([-_np.sin(angle), _np.sin(angle)]).astype(_np.float32))
    spill = nc.dram_tensor("x1_spill", (seq, 512), _mybir.dt.float32, kind="Internal").ap()
    out = nc.dram_tensor("out_0_dram", (2, 1024, 512), _mybir.dt.float32, kind="ExternalOutput").ap()
    adaln_block(nc, *args, spill, out)
    r = _run(nc, [arrays], core_ids=[0])
    return r.results[0]["out_0_dram"]
```
